# Optimizing a Trainium2 kernel written in Bass

```python
import numpy as np
import jax
import jax.numpy as jnp

def _softmax(x, axis=-1):
    return jax.nn.softmax(x, axis=axis)

def _gelu(x):
    return jax.nn.gelu(x, approximate=True)

def _silu(x):
    return jax.nn.silu(x)

def _sigmoid(x):
    return jax.nn.sigmoid(x)

def _layernorm(x, axis=-1, eps=1e-05):
    m = jnp.mean(x, axis=axis, keepdims=True)
    v = jnp.var(x, axis=axis, keepdims=True)
    return (x - m) / jnp.sqrt(v + eps)

def _scatter_add(tgt, idx, src, axis=0):
    return tgt.at[idx].add(src)

def _segment_sum(src, seg, n):
    return jax.ops.segment_sum(src, seg, n)
kernel_name = 'mk_adj_preln_d2_adj_r2_7664bc'

def setup_inputs(seed: int=0):
    np.random.seed(seed)
    _w = jnp.asarray

    def _rec_inputs():
        import jax
        import jax.numpy as jnp
        _gk = jax.random.key(seed)
        x = 7.22e-05 + 1 * jax.random.normal(jax.random.fold_in(_gk, 1), (2048, 512), jnp.float32)
        _a = jax.random.bernoulli(jax.random.fold_in(_gk, 2), 0.0078125, (2048, 2048))
        _a = jnp.logical_or(_a, jnp.swapaxes(_a, -1, -2))
        _a = jnp.logical_or(_a, jnp.eye(2048, dtype=bool))
        _af = _a.astype(jnp.float32)
        _af = _af * jax.random.uniform(jax.random.fold_in(_gk, 3), (2048, 2048), jnp.float32, 0.05, 1)
        adj = _af
        return (x, adj)
    x, adj = _rec_inputs()

    def _L0_gnn_setup():
        import jax, jax.numpy as jnp
        import numpy as np
        N = 4096
        IN_FEATURES = 512
        OUT_FEATURES = 512
        key = jax.random.key(seed)
        k_x, k_adj, k_w, k_b = jax.random.split(key, 4)
        x = jax.random.normal(k_x, (N, IN_FEATURES), dtype=jnp.float32)
        adj = jax.random.uniform(k_adj, (N, N), dtype=jnp.float32)
        stdv = 1.0 / np.sqrt(OUT_FEATURES)
        weight = jax.random.uniform(k_w, (IN_FEATURES, OUT_FEATURES), dtype=jnp.float32, minval=-stdv, maxval=stdv)
        bias = jax.random.uniform(k_b, (OUT_FEATURES,), dtype=jnp.float32, minval=-stdv, maxval=stdv)
        return {'x': x, 'adj': adj, 'weight': weight, 'bias': bias}
    _L0_gnn_all = _L0_gnn_setup()
    _L0_gnn_in = {k: v for k, v in _L0_gnn_all.items() if k in ('weight', 'bias')}
    del _L0_gnn_all

    def _L1_gnn_setup():
        import jax, jax.numpy as jnp
        import numpy as np
        N = 4096
        D = 512

        def adjacent_mat(adj):
            adj = adj + jnp.eye(adj.shape[0], dtype=adj.dtype)
            deg = jnp.sum(adj, axis=1)
            dinv = jnp.where(deg > 0, deg ** (-0.5), 0.0).astype(adj.dtype)
            return dinv[:, None] * adj * dinv[None, :]
        key = jax.random.key(seed)
        k1, k2 = jax.random.split(key)
        x = jax.random.normal(k1, (N, D), dtype=jnp.float32)
        Coefficient2 = 1e-08 * jnp.ones((N, N), dtype=jnp.float32)
        A = jax.random.uniform(k2, (N, N), dtype=jnp.float32)
        return {'x': x, 'Coefficient2': Coefficient2, 'A': A}
    _L1_gnn_all = _L1_gnn_setup()
    _L1_gnn_in = {k: v for k, v in _L1_gnn_all.items() if k in ()}
    del _L1_gnn_all
    return {'x': x, 'adj': adj, 'L0_gnn_weight': _L0_gnn_in['weight'], 'L0_gnn_bias': _L0_gnn_in['bias']}

def reference(x, adj, L0_gnn_weight, L0_gnn_bias):
    import jax
    import jax.numpy as jnp

    def _L0_gnn_ref(x, adj, weight, bias):
        import jax, jax.numpy as jnp
        import numpy as np
        N = 4096
        IN_FEATURES = 512
        OUT_FEATURES = 512
        support = jnp.matmul(x, weight)
        output = jnp.matmul(adj, support)
        return output + bias

    def _L1_gnn_ref(x, Coefficient2, A):
        import jax, jax.numpy as jnp
        import numpy as np
        N = 4096
        D = 512

        def adjacent_mat(adj):
            adj = adj + jnp.eye(adj.shape[0], dtype=adj.dtype)
            deg = jnp.sum(adj, axis=1)
            dinv = jnp.where(deg > 0, deg ** (-0.5), 0.0).astype(adj.dtype)
            return dinv[:, None] * adj * dinv[None, :]
        A_c = jax.lax.stop_gradient(A)
        adj = adjacent_mat((A_c + A_c.T) * 0.5)
        y = Coefficient2 @ adj
        y = y @ x
        return y
    h = jnp.maximum(_layernorm(x, axis=-1), 0.0)
    x = x + _L0_gnn_ref(h, adj, L0_gnn_weight, L0_gnn_bias)
    h = jnp.maximum(_layernorm(x, axis=-1), 0.0)
    x = x + _L1_gnn_ref(h, adj, adj)
    return x

_drawn_inputs = setup_inputs


def setup_inputs(seed=0):
    import zlib

    import numpy as np

    out = dict(_drawn_inputs(seed))
    spreads = {}
    factors = {'L0_gnn_bias': 8.0}
    for name, (base, spread) in spreads.items():
        noise = np.random.default_rng([zlib.crc32(name.encode()), seed]).standard_normal(out[name].shape)
        drawn = base * np.exp(spread * noise) if base else spread * noise
        out[name] = jnp.asarray(drawn.astype(out[name].dtype))
    for name, factor in factors.items():
        out[name] = (out[name] * factor).astype(out[name].dtype)
    return out
```

```python
import concourse.bass as bass
from concourse import mybir
from contextlib import ExitStack


def two_layer_graph_conv(nc, x, adj, weight, bias, adj_t_blocks, out):
    fp32 = mybir.dt.float32
    fp32r = mybir.dt.float32r
    ALU = mybir.AluOpType
    ACT = mybir.ActivationFunctionType
    AX = mybir.AxisListType

    P = 128
    N, D = x.shape
    NT = N // P
    ND = D // P
    Q = NT // ND
    EPS = 1e-5
    L2, L3, END = NT, 2 * NT, 3 * NT

    x_tiles = x.rearrange("(t p) d -> p t d", p=P)
    out_tiles = out.rearrange("(t p) d -> p t d", p=P)
    adj_rows = adj.rearrange("(t p) k -> t p k", p=P)
    adj_cols = adj.rearrange("(k p) (t m) -> t p k m", p=P, m=P)

    ctx = ExitStack()
    with ctx:
        def sb(name, shape, dt=fp32):
            return ctx.enter_context(nc.sbuf_tensor(name, shape, dt))

        def sem(name):
            return ctx.enter_context(nc.semaphore(name))

        act_hi = sb("act_hi", [P, NT, D], fp32r)
        act_lo = sb("act_lo", [P, NT, D], fp32r)
        nxt = sb("nxt", [P, NT, D])
        res = sb("res", [P, NT, D])
        blk_hi = sb("blk_hi", [P, 2, NT, P], fp32r)
        blk_lo = sb("blk_lo", [P, 2, NT, P], fp32r)
        nat = sb("nat", [P, 2, N])
        tr = sb("tr", [P, 2, N])
        hT_hi = sb("hT_hi", [P, 2, D], fp32r)
        hT_lo = sb("hT_lo", [P, 2, D], fp32r)
        ident = sb("ident", [P, P])
        ident2 = sb("ident2", [P, P])
        row_buf = sb("row_buf", [P, D])
        row_sum = sb("row_sum", [P, NT])
        col_part = sb("col_part", [P, NT, NT])
        col_sum = sb("col_sum", [P, NT])
        dinv = sb("dinv", [P, NT])
        half_dinv = sb("half_dinv", [P, NT])
        deg = sb("deg", [P, NT])
        deg_pos = sb("deg_pos", [P, NT])
        deg_c = sb("deg_c", [P, NT])
        deg_t = sb("deg_t", [P, 4, NT])
        stats = sb("stats", [P, 2, 6])
        mv = sb("mv", [P, 2, 2])
        ln_t = sb("ln_t", [P, 5, 2])
        rstd = sb("rstd", [P, 2])
        shift = sb("shift", [P, 2])

        acc = ctx.enter_context(nc.psum_tensor("acc", [P, 2, D], fp32))
        tp = ctx.enter_context(nc.psum_tensor("tp", [P, Q, 4 * P], fp32))
        tph = ctx.enter_context(nc.psum_tensor("tph", [P, 2, D], fp32))

        x_in = nxt[:, 4:8, :]
        w_raw = nat[:, 1, 0:ND * D]
        w_hi = blk_hi[:, 1, :, :].rearrange("p k m -> p (k m)")
        w_lo = blk_lo[:, 1, :, :].rearrange("p k m -> p (k m)")

        def blk(t, par):
            return t[:, par, :, :].rearrange("p k m -> p (k m)")

        s_x = [sem("s_x0"), sem("s_x1_loaded")]
        s_w = sem("s_w_loaded")
        s_bias = sem("s_bias_loaded")
        s_ident = sem("s_ident")
        s_whi = sem("s_w_hi")
        s_wlo = sem("s_w_lo")
        s_xb = sem("s_x_plus_bias")
        s_var = sem("s_var_ready")
        s_root = sem("s_root_ready")
        s_norm = sem("s_norm_ready")
        s_h = sem("s_h_ready")
        s_hT = sem("s_hT_psum")
        s_hThi = sem("s_hT_hi")
        s_hTlo = sem("s_hT_lo")
        s_sup = sem("s_support_psum")
        s_ahi = sem("s_act_hi")
        s_alo = sem("s_act_lo")
        s_used = sem("s_act_used")
        s_nat = [sem("s_nat0"), sem("s_nat1")]
        s_tr = [sem("s_tr0"), sem("s_tr1")]
        s_keep = [sem("s_keep0"), sem("s_keep1")]
        s_tp = sem("s_transposed")
        s_raw = sem("s_raw")
        s_rsum = sem("s_row_sum")
        s_csum = sem("s_col_sum")
        s_sadd = sem("s_sum_added")
        s_sym = sem("s_sym")
        s_bhi = sem("s_blk_hi")
        s_blo = sem("s_blk_lo")
        s_acc = sem("s_acc_done")
        s_x1 = sem("s_x1")
        s_res = sem("s_res")
        s_h1 = sem("s_h1")
        s_z = sem("s_z")
        s_o = sem("s_o")
        s_dvar = sem("s_deg_ready")
        s_droot = sem("s_deg_root")
        s_dinv = sem("s_dinv")
        s_ch = sem("s_dve_chain")
        s_out = sem("s_out")

        block = ctx.enter_context(nc.Block())

        @block.sync
        def _(sp):
            def load_x(j, par):
                sp.dma_start(x_in[:, 2 * par:2 * par + 2, :], x_tiles[:, bass.ds(2 * j, 2), :]).then_inc(s_x[par], 16)

            def reload_x(j, par):
                sp.wait_ge(s_h, 2 * j - 2)
                sp.wait_ge(s_xb, 2 * j - 2)
                load_x(j, par)

            load_x(0, 0)
            sp.dma_start(w_raw.rearrange("p (c n) -> p c n", c=ND),
                         weight.rearrange("(c p) n -> p c n", p=P)).then_inc(s_w, 16)
            load_x(1, 1)
            sp.dma_start(row_buf[:, :], bias.rearrange("(a n) -> a n", a=1).broadcast_to([P, D])).then_inc(s_bias, 16)
            with sp.Fori(1, NT // 4) as i:
                reload_x(2 * i, 0)
                reload_x(2 * i + 1, 1)

            def load_rows(t, par):
                sp.dma_start(nat[:, par, :], adj_rows[t, :, :]).then_inc(s_nat[par], 16)

            load_rows(0, 0)
            sp.wait_ge(s_whi, 1)
            sp.wait_ge(s_wlo, 1)
            load_rows(1, 1)

            def layer1(t, par, more):
                if more:
                    sp.wait_ge(s_tp, Q * (t + 1))
                    sp.wait_ge(s_rsum, t + 1)
                    load_rows(t + 2, par)
                sp.wait_ge(s_raw, Q * (t + 1))
                sp.dma_start(adj_t_blocks[t, :, :], tr[:, par, :]).then_inc(s_keep[par], 16)

            with sp.Fori(0, NT // 2 - 1) as i:
                layer1(2 * i, 0, True)
                layer1(2 * i + 1, 1, True)
            layer1(NT - 2, 0, False)
            layer1(NT - 1, 1, False)

            def load_cols(u, par):
                sp.dma_start(nat[:, par, :].rearrange("p (k m) -> p k m", m=P), adj_cols[u, :, :, :])\
                  .then_inc(s_nat[par], 16)

            def load_tr(u, par):
                sp.dma_start(tr[:, par, :], adj_t_blocks[u, :, :]).then_inc(s_tr[par], 16)

            for par in range(2):
                sp.wait_ge(s_tp, Q * (NT - 1 + par))
                sp.wait_ge(s_rsum, NT - 1 + par)
                load_cols(par, par)
                sp.wait_ge(s_keep[par], 16 * (NT // 2))
                sp.wait_ge(s_csum, NT - 1 + par)
                sp.wait_ge(s_blo, NT - 1 + par)
                load_tr(par, par)

            def layer2(u, par):
                sp.wait_ge(s_sadd, u - 1)
                load_cols(u, par)
                sp.wait_ge(s_blo, L2 + u - 1)
                load_tr(u, par)

            with sp.Fori(1, NT // 2) as i:
                layer2(2 * i, 0)
                layer2(2 * i + 1, 1)

            def store(v):
                sp.wait_ge(s_o, v + 1)
                sp.dma_start(out_tiles[:, v, :], res[:, v, :]).then_inc(s_out, 16)

            def layer3(v, par):
                sp.wait_ge(s_blo, L3 + v - 1)
                load_tr(v, par)

            layer3(0, 0)
            layer3(1, 1)
            layer3(2, 0)
            with sp.Fori(0, NT // 2 - 2) as i:
                layer3(2 * i + 3, 1)
                store(2 * i)
                layer3(2 * i + 4, 0)
                store(2 * i + 1)
            layer3(NT - 1, 1)
            with sp.Fori(NT - 4, NT) as v:
                store(v)
            sp.wait_ge(s_out, 16 * NT)

        @block.gpsimd
        def _(pool):
            for m in (ident, ident2):
                nc.gpsimd.memset(m[:, :], 0.0).then_inc(s_ident, 1)
            pool.wait_ge(s_ident, 2)
            for m, v in ((ident, 1.0), (ident2, 2.0)):
                nc.gpsimd.affine_select(out=m[:, :], in_=m[:, :], compare_op=ALU.not_equal, fill=v,
                                        base=0, pattern=[[-1, P]], channel_multiplier=1).then_inc(s_ident, 1)
            pool.wait_ge(s_bias, 16)
            def add_bias(t, slot, j):
                pool.wait_ge(s_x[slot // 2], 16 * (j + 1))
                nc.gpsimd.tensor_tensor(res[:, t, :], x_in[:, slot, :], row_buf[:, :], ALU.add).then_inc(s_xb, 1)

            with pool.Fori(0, NT // 4) as i:
                for slot in range(4):
                    add_bias(4 * i + slot, slot, i)
            with pool.Fori(0, NT) as t:
                pool.wait_ge(s_x1, t + 1)
                nc.gpsimd.tensor_copy(res[:, t, :], row_buf[:, :]).then_inc(s_res, 1)

        @block.tensor
        def _(pe):
            def product(dst, w, a, first, last):
                nc.tensor.matmul(dst, w[0], a[0], start=first, stop=False)
                nc.tensor.matmul(dst, w[0], a[1], start=False, stop=False)
                return nc.tensor.matmul(dst, w[1], a[0], start=False, stop=last)

            def transpose_h(t, par, reused=True):
                pe.wait_ge(s_h, t + 1)
                if reused:
                    pe.wait_ge(s_hTlo, t - 1)
                for c in range(ND):
                    ins = nc.tensor.transpose(tph[:, par, c * P:(c + 1) * P],
                                              nxt[:, par, c * P:(c + 1) * P], ident[:, :])
                ins.then_inc(s_hT, 1)

            def support(t, par, reused=True):
                pe.wait_ge(s_hThi, t + 1)
                pe.wait_ge(s_hTlo, t + 1)
                if reused:
                    pe.wait_ge(s_alo, t - 1)
                for c in range(ND):
                    k, n = slice(c * P, (c + 1) * P), slice(c * D, (c + 1) * D)
                    ins = product(acc[:, par, :], (hT_hi[:, par, k], hT_lo[:, par, k]),
                                  (w_hi[:, n], w_lo[:, n]), c == 0, c == ND - 1)
                ins.then_inc(s_sup, 1)

            def transpose_rows(t, par, j, reused=True):
                pe.wait_ge(s_nat[par], 16 * (j + 1))
                for q in range(Q):
                    if reused:
                        pe.wait_ge(s_raw, Q * (t - 1) + q + 1)
                    for b in range(NT // Q):
                        k = q * (NT // Q) + b
                        ins = nc.tensor.transpose(tp[:, q, b * P:(b + 1) * P],
                                                  nat[:, par, k * P:(k + 1) * P], ident[:, :])
                    ins.then_inc(s_tp, 1)

            def aggregate(tile, par, free=None, fresh=None, release=False):
                pe.wait_ge(s_bhi, tile + 1)
                pe.wait_ge(s_blo, tile + 1)
                if free is not None:
                    pe.wait_ge(*free)
                for k in range(NT):
                    if fresh is not None:
                        pe.wait_ge(s_ahi, fresh + k + 1)
                        pe.wait_ge(s_alo, fresh + k + 1)
                    ins = product(acc[:, par, :], (blk_hi[:, par, k, :], blk_lo[:, par, k, :]),
                                  (act_hi[:, k, :], act_lo[:, k, :]), k == 0, k == NT - 1)
                    if release and k < NT - 1:
                        ins.then_inc(s_used, 1)
                ins.then_inc(s_acc, 1)

            pe.wait_ge(s_ident, 4)
            transpose_h(0, 0, False)
            transpose_h(1, 1, False)
            pe.wait_ge(s_whi, 1)
            pe.wait_ge(s_wlo, 1)
            support(0, 0, False)
            transpose_h(2, 0)
            support(1, 1, False)
            with pe.Fori(0, NT // 2 - 3) as i:
                transpose_h(2 * i + 3, 1)
                support(2 * i + 2, 0)
                transpose_h(2 * i + 4, 0)
                support(2 * i + 3, 1)
            transpose_h(NT - 3, 1)
            support(NT - 4, 0)
            transpose_h(NT - 2, 0)
            transpose_rows(0, 0, 0, False)
            support(NT - 3, 1)
            transpose_h(NT - 1, 1)
            support(NT - 2, 0)
            support(NT - 1, 1)

            transpose_rows(1, 1, 0)
            aggregate(0, 0, (s_alo, NT - 1), fresh=0)
            transpose_rows(2, 0, 1)
            aggregate(1, 1)
            with pe.Fori(0, NT // 2 - 2) as i:
                transpose_rows(2 * i + 3, 1, i + 1)
                aggregate(2 * i + 2, 0, (s_x1, 2 * i + 1))
                transpose_rows(2 * i + 4, 0, i + 2)
                aggregate(2 * i + 3, 1, (s_x1, 2 * i + 2))
            transpose_rows(NT - 1, 1, NT // 2 - 1)
            aggregate(NT - 2, 0, (s_x1, NT - 3))
            aggregate(NT - 1, 1, (s_x1, NT - 2), release=True)

            aggregate(L2, 0, (s_x1, NT - 1), fresh=NT)
            aggregate(L2 + 1, 1, (s_x1, NT))
            with pe.Fori(0, NT // 2 - 2) as i:
                aggregate(L2 + 2 * i + 2, 0, (s_z, 2 * i + 1))
                aggregate(L2 + 2 * i + 3, 1, (s_z, 2 * i + 2))
            aggregate(L3 - 2, 0, (s_z, NT - 3))
            aggregate(L3 - 1, 1, (s_z, NT - 2), release=True)

            aggregate(L3, 0, (s_z, NT - 1), fresh=2 * NT)
            aggregate(L3 + 1, 1, (s_z, NT))
            with pe.Fori(0, NT // 2 - 1) as i:
                aggregate(L3 + 2 * i + 2, 0, (s_o, 2 * i + 1))
                aggregate(L3 + 2 * i + 3, 1, (s_o, 2 * i + 2))

        @block.scalar
        def _(act):
            def root(n, cols):
                act.wait_ge(s_var, n + 1)
                nc.scalar.activation(ln_t[:, 1, 0:cols], ln_t[:, 0, 0:cols], ACT.Sqrt).then_inc(s_root, 1)

            def normalize(t, slot, pair, reused=True):
                par = slot % 2
                act.wait_ge(s_norm, pair + 1)
                if reused:
                    act.wait_ge(s_hT, t - 1)
                nc.scalar.activation(nxt[:, par, :], x_in[:, slot, :], ACT.Relu, scale=rstd[:, par:par + 1],
                                     bias=shift[:, par:par + 1]).then_inc(s_h, 1)

            def split_hT(t, par, reused=True):
                act.wait_ge(s_hT, t + 1)
                if reused:
                    act.wait_ge(s_sup, t - 1)
                nc.scalar.copy(hT_hi[:, par, :], tph[:, par, :]).then_inc(s_hThi, 1)

            def split_support(t, par):
                act.wait_ge(s_sup, t + 1)
                nc.scalar.copy(act_hi[:, t, :], acc[:, par, :]).then_inc(s_ahi, 1)

            def copy_rows(t, par, keeps=None):
                if keeps is not None:
                    act.wait_ge(s_keep[par], 16 * keeps)
                    act.wait_ge(s_csum, t - 1)
                    act.wait_ge(s_blo, t - 1)
                for q in range(Q):
                    act.wait_ge(s_tp, Q * t + q + 1)
                    nc.scalar.copy(tr[:, par, q * D:(q + 1) * D], tp[:, q, :]).then_inc(s_raw, 1)

            def split_block(tile, par, ready, used=None):
                act.wait_ge(*ready)
                if used is not None:
                    act.wait_ge(s_acc, used)
                nc.scalar.copy(blk(blk_hi, par), tr[:, par, :]).then_inc(s_bhi, 1)

            def normalize1(t):
                root(NT // 2 + t, 1)
                act.wait_ge(s_norm, NT // 2 + t + 1)
                nc.scalar.activation(nxt[:, t, :], row_buf[:, :], ACT.Relu, scale=rstd[:, 0:1],
                                     bias=shift[:, 0:1]).then_inc(s_h1, 1)

            root(0, 2)
            normalize(0, 0, 0, False)
            normalize(1, 1, 0, False)
            act.wait_ge(s_w, 16)
            nc.scalar.copy(w_hi, w_raw).then_inc(s_whi, 1)
            root(1, 2)
            split_hT(0, 0, False)

            def prepare(i, pair, norm, roots):
                if norm:
                    normalize(2 * i + 2, 2 * pair, i + 1)
                split_hT(2 * i + 1, 1, not isinstance(i, int) or i > 0)
                split_support(2 * i, 0)
                if norm:
                    normalize(2 * i + 3, 2 * pair + 1, i + 1)
                split_hT(2 * i + 2, 0)
                if roots:
                    root(i + 2, 2)

            prepare(0, 1, True, True)
            split_support(1, 1)
            with act.Fori(0, NT // 4 - 2) as i:
                prepare(2 * i + 1, 0, True, True)
                split_support(4 * i + 3, 1)
                prepare(2 * i + 2, 1, True, True)
                split_support(4 * i + 5, 1)
            prepare(NT // 2 - 3, 0, True, True)
            split_support(NT - 5, 1)
            prepare(NT // 2 - 2, 1, True, False)
            copy_rows(0, 0)
            split_support(NT - 3, 1)
            split_hT(NT - 1, 1)
            split_block(0, 0, (s_raw, Q))
            split_support(NT - 2, 0)
            split_support(NT - 1, 1)

            copy_rows(1, 1)
            split_block(1, 1, (s_raw, 2 * Q), 0)
            normalize1(0)
            with act.Fori(0, NT // 2 - 1) as i:
                copy_rows(2 * i + 2, 0, i + 1)
                split_block(2 * i + 2, 0, (s_raw, Q * (2 * i + 3)), 2 * i + 1)
                normalize1(2 * i + 1)
                copy_rows(2 * i + 3, 1, i + 1)
                split_block(2 * i + 3, 1, (s_raw, Q * (2 * i + 4)), 2 * i + 2)
                normalize1(2 * i + 2)

            act.wait_ge(s_dvar, 1)
            nc.scalar.activation(deg_t[:, 0, :], deg_c[:, :], ACT.Sqrt).then_inc(s_droot, 1)
            split_block(L2, 0, (s_sym, 1), NT - 1)
            act.wait_ge(s_dinv, 1)
            act.wait_ge(s_h1, NT - 1)
            for k in range(NT):
                if k == NT - 1:
                    normalize1(k)
                    act.wait_ge(s_h1, NT)
                    act.wait_ge(s_acc, NT)
                else:
                    act.wait_ge(s_used, k + 1)
                nc.scalar.activation(act_hi[:, k, :], nxt[:, k, :], ACT.Copy, scale=dinv[:, k:k + 1])\
                  .then_inc(s_ahi, 1)

            def take_z(u, par):
                act.wait_ge(s_acc, L2 + u + 1)
                nc.scalar.activation(nxt[:, u, :], acc[:, par, :], ACT.Copy,
                                     scale=half_dinv[:, bass.ds(u, 1)]).then_inc(s_z, 1)

            split_block(L2 + 1, 1, (s_sym, 2), NT)
            act.wait_ge(s_alo, 2 * NT)
            take_z(0, 0)
            with act.Fori(0, NT // 2 - 1) as i:
                split_block(L2 + 2 * i + 2, 0, (s_sym, 2 * i + 3), L2 + 2 * i + 1)
                take_z(2 * i + 1, 1)
                split_block(L2 + 2 * i + 3, 1, (s_sym, 2 * i + 4), L2 + 2 * i + 2)
                take_z(2 * i + 2, 0)

            loads = NT // 2
            split_block(L3, 0, (s_tr[0], 16 * (loads + 1)), L3 - 1)
            act.wait_ge(s_z, NT - 1)
            for k in range(NT):
                if k == NT - 1:
                    take_z(k, 1)
                    act.wait_ge(s_z, NT)
                else:
                    act.wait_ge(s_used, NT - 1 + k + 1)
                nc.scalar.copy(act_hi[:, k, :], nxt[:, k, :]).then_inc(s_ahi, 1)

            split_block(L3 + 1, 1, (s_tr[1], 16 * (loads + 1)), L3)
            with act.Fori(0, NT // 2 - 1) as i:
                split_block(L3 + 2 * i + 2, 0, (s_tr[0], 16 * (loads + 2 + i)), L3 + 2 * i + 1)
                split_block(L3 + 2 * i + 3, 1, (s_tr[1], 16 * (loads + 2 + i)), L3 + 2 * i + 2)

        @block.vector
        def _(dve):
            STATS, NORM = 2, 4

            def chained(ins, n):
                ins.then_inc(s_ch, 1)
                dve.wait_ge(s_ch, n)

            def tile_stats(tile, col, n):
                dve.nop(nofuse=True)
                chained(nc.vector.bn_stats(stats[:, col, :], tile), n + 1)
                dve.nop(nofuse=True)
                chained(nc.vector.bn_aggr(mv[:, col, :], stats[:, col, :]), n + 2)

            def variance(cols):
                nc.vector.tensor_scalar(ln_t[:, 0, 0:cols], mv[:, 0:cols, 1], EPS, None, ALU.add)\
                  .then_inc(s_var, 1)

            def inv_root(out_, v, r, a, b, n):
                chained(nc.vector.reciprocal(r, r), n + 1)
                chained(nc.vector.tensor_tensor(a, r, r, ALU.mult), n + 2)
                chained(nc.vector.scalar_tensor_tensor(b, a, -0.5, v, ALU.mult, ALU.mult), n + 3)
                chained(nc.vector.scalar_tensor_tensor(out_, b, 1.5, r, ALU.add, ALU.mult), n + 4)

            def norm(step, cols, n):
                dve.wait_ge(s_root, step + 1)
                inv_root(rstd[:, 0:cols], ln_t[:, 0, 0:cols], ln_t[:, 1, 0:cols], ln_t[:, 3, 0:cols],
                         ln_t[:, 4, 0:cols], n)
                nc.vector.scalar_tensor_tensor(shift[:, 0:cols], mv[:, 0:cols, 0], -1.0, rstd[:, 0:cols],
                                               ALU.mult, ALU.mult).then_inc(s_norm, 1)

            PAIR = 2 * STATS + NORM
            TILE = STATS + NORM
            BASE1 = (NT // 2) * PAIR

            def split_hT(t, par):
                dve.wait_ge(s_hThi, t + 1)
                nc.vector.tensor_tensor(hT_lo[:, par, :], tph[:, par, :], hT_hi[:, par, :].bitcast(fp32),
                                        ALU.subtract).then_inc(s_hTlo, 1)

            def split_support(t, par):
                dve.wait_ge(s_ahi, t + 1)
                nc.vector.tensor_tensor(act_lo[:, t, :], acc[:, par, :], act_hi[:, t, :].bitcast(fp32),
                                        ALU.subtract).then_inc(s_alo, 1)

            def sum_rows(t, par, j):
                dve.wait_ge(s_nat[par], 16 * (j + 1))
                nc.vector.tensor_reduce(row_sum[:, bass.ds(t, 1)], nat[:, par, :], AX.X, ALU.add)\
                  .then_inc(s_rsum, 1)

            def sum_cols(t, par):
                dve.wait_ge(s_raw, Q * (t + 1))
                nc.vector.tensor_reduce(col_part[:, :, bass.ds(t, 1)],
                                        tr[:, par, :].rearrange("p (k m) -> p k m", m=P), AX.X, ALU.add)\
                  .then_inc(s_csum, 1)

            def split_block(tile, par):
                dve.wait_ge(s_bhi, tile + 1)
                nc.vector.tensor_tensor(blk(blk_lo, par), tr[:, par, :], blk(blk_hi, par).bitcast(fp32),
                                        ALU.subtract).then_inc(s_blo, 1)

            def take_x1(t, par, n):
                dve.wait_ge(s_acc, t + 1)
                if not isinstance(t, int) or t > 0:
                    dve.wait_ge(s_h1, t)
                    dve.wait_ge(s_res, t)
                nc.vector.tensor_tensor(row_buf[:, :], acc[:, par, :], res[:, t, :], ALU.add).then_inc(s_x1, 1)
                dve.wait_ge(s_x1, t + 1)
                tile_stats(row_buf[:, :], 0, n)
                variance(1)
                norm(NT // 2 + t, 1, n + STATS)

            for j in range(2):
                dve.wait_ge(s_x[j], 16)
                tile_stats(x_in[:, 2 * j, :], 0, PAIR * j)
                tile_stats(x_in[:, 2 * j + 1, :], 1, PAIR * j + STATS)
                variance(2)
                norm(j, 2, PAIR * j + 2 * STATS)
                if j == 0:
                    dve.wait_ge(s_whi, 1)
                    nc.vector.tensor_tensor(w_lo, w_raw, w_hi.bitcast(fp32), ALU.subtract).then_inc(s_wlo, 1)
            split_hT(0, 0)

            def prepare(i, par, j):
                dve.wait_ge(s_x[par], 16 * (j + 1))
                tile_stats(x_in[:, 2 * par, :], 0, PAIR * (i + 2))
                split_hT(2 * i + 1, 1)
                split_support(2 * i, 0)
                tile_stats(x_in[:, 2 * par + 1, :], 1, PAIR * (i + 2) + STATS)
                variance(2)
                split_hT(2 * i + 2, 0)
                split_support(2 * i + 1, 1)
                norm(i + 2, 2, PAIR * (i + 2) + 2 * STATS)

            with dve.Fori(0, NT // 4 - 1) as i:
                prepare(2 * i, 0, i + 1)
                prepare(2 * i + 1, 1, i + 1)
            split_hT(NT - 3, 1)
            split_support(NT - 4, 0)
            split_hT(NT - 2, 0)
            sum_rows(0, 0, 0)
            split_support(NT - 3, 1)
            split_hT(NT - 1, 1)
            split_block(0, 0)
            split_support(NT - 2, 0)
            split_support(NT - 1, 1)

            dve.wait_ge(s_xb, NT)
            sum_cols(0, 0)
            sum_rows(1, 1, 0)
            sum_cols(1, 1)
            split_block(1, 1)
            take_x1(0, 0, BASE1)
            with dve.Fori(0, NT // 2 - 1) as i:
                sum_rows(2 * i + 2, 0, i + 1)
                sum_cols(2 * i + 2, 0)
                split_block(2 * i + 2, 0)
                take_x1(2 * i + 1, 1, BASE1 + TILE * (2 * i + 1))
                sum_rows(2 * i + 3, 1, i + 1)
                sum_cols(2 * i + 3, 1)
                split_block(2 * i + 3, 1)
                take_x1(2 * i + 2, 0, BASE1 + TILE * (2 * i + 2))

            n = BASE1 + TILE * (NT - 1)
            dve.wait_ge(s_csum, NT)
            dve.wait_ge(s_rsum, NT)
            chained(nc.vector.tensor_reduce(col_sum[:, :], col_part[:, :, :], AX.X, ALU.add), n + 1)
            chained(nc.vector.tensor_tensor(deg[:, :], row_sum[:, :], col_sum[:, :], ALU.add), n + 2)
            chained(nc.vector.tensor_scalar(deg[:, :], deg[:, :], 0.5, 1.0, ALU.mult, ALU.add), n + 3)
            nc.vector.tensor_scalar(deg_pos[:, :], deg[:, :], 0.0, None, ALU.is_gt)
            nc.vector.tensor_scalar(deg_c[:, :], deg[:, :], 2.0 ** -100, None, ALU.max).then_inc(s_dvar, 1)

            def symmetric(u, par, j):
                dve.wait_ge(s_nat[par], 16 * (NT // 2 + j + 1))
                dve.wait_ge(s_tr[par], 16 * (j + 1))
                nc.vector.tensor_tensor(tr[:, par, :], tr[:, par, :], nat[:, par, :], ALU.add).then_inc(s_sadd, 1)
                dve.wait_ge(s_sadd, u + 1)
                diag = tr[:, par, bass.ds(P * u, P)]
                nc.vector.tensor_tensor(diag, diag, ident2[:, :], ALU.add).then_inc(s_sym, 1)

            symmetric(0, 0, 0)
            dve.wait_ge(s_droot, 1)
            inv_root(deg_t[:, 1, :], deg_c[:, :], deg_t[:, 0, :], deg_t[:, 2, :], deg_t[:, 3, :], n + 3)
            chained(nc.vector.tensor_tensor(dinv[:, :], deg_t[:, 1, :], deg_pos[:, :], ALU.mult), n + 8)
            nc.vector.tensor_scalar(half_dinv[:, :], dinv[:, :], 0.5, None, ALU.mult).then_inc(s_dinv, 1)
            split_block(L2, 0)
            symmetric(1, 1, 0)
            for k in range(NT):
                if k == NT - 1:
                    take_x1(k, 1, n + 8)
                dve.wait_ge(s_ahi, NT + k + 1)
                nc.vector.scalar_tensor_tensor(act_lo[:, k, :], nxt[:, k, :], dinv[:, k:k + 1],
                                               act_hi[:, k, :].bitcast(fp32), ALU.mult, ALU.subtract)\
                  .then_inc(s_alo, 1)
            split_block(L2 + 1, 1)
            with dve.Fori(0, NT // 2 - 1) as i:
                symmetric(2 * i + 2, 0, i + 1)
                split_block(L2 + 2 * i + 2, 0)
                symmetric(2 * i + 3, 1, i + 1)
                split_block(L2 + 2 * i + 3, 1)

            split_block(L3, 0)
            for k in range(NT):
                dve.wait_ge(s_ahi, L3 + k + 1)
                nc.vector.tensor_tensor(act_lo[:, k, :], nxt[:, k, :], act_hi[:, k, :].bitcast(fp32),
                                        ALU.subtract).then_inc(s_alo, 1)

            def take_out(v, par):
                dve.wait_ge(s_acc, L3 + v + 1)
                nc.vector.tensor_tensor(res[:, v, :], acc[:, par, :], res[:, v, :], ALU.add).then_inc(s_o, 1)

            split_block(L3 + 1, 1)
            dve.wait_ge(s_res, NT)
            take_out(0, 0)
            with dve.Fori(0, NT // 2 - 1) as i:
                split_block(L3 + 2 * i + 2, 0)
                take_out(2 * i + 1, 1)
                split_block(L3 + 2 * i + 3, 1)
                take_out(2 * i + 2, 0)
            take_out(NT - 1, 1)


_INS = ['x', 'adj', 'L0_gnn_weight', 'L0_gnn_bias']


def kernel(**inputs):
    import numpy as _np
    import concourse.bacc as _bacc
    from concourse import mybir as _mybir
    from concourse.bass_utils import run_bass_kernel_spmd as _run

    nc = _bacc.Bacc("TRN2", target_bir_lowering=False, num_devices=1)
    arrays, args = {}, []
    for name in _INS:
        a = _np.ascontiguousarray(inputs[name])
        arrays[f"in_{name}_dram"] = a
        args.append(nc.dram_tensor(f"in_{name}_dram", a.shape, _mybir.dt.from_np(a.dtype), kind="ExternalInput").ap())
    shape = inputs['x'].shape
    rows = inputs['adj'].shape[0]
    kept = nc.dram_tensor("adj_t_blocks", (rows // 128, 128, rows), _mybir.dt.float32, kind="Internal").ap()
    result = nc.dram_tensor("out_dram", shape, _mybir.dt.float32, kind="ExternalOutput").ap()
    two_layer_graph_conv(nc, *args, kept, result)
    r = _run(nc, [arrays], core_ids=[0])
    return r.results[0]["out_dram"]
```

```python
import concourse.bass as bass
from concourse import mybir
from contextlib import ExitStack


def two_layer_graph_conv(nc, x, adj, weight, bias, adj_t_blocks, out):
    fp32 = mybir.dt.float32
    fp32r = mybir.dt.float32r
    ALU = mybir.AluOpType
    ACT = mybir.ActivationFunctionType
    AX = mybir.AxisListType

    P = 128
    B = 32
    G = P // B
    N, D = x.shape
    NT = N // P
    ND = D // P
    W = N // G
    H = NT // 2
    S = 4
    EPS = 1e-5
    SPLIT2, SPLIT3 = NT, NT + 2 * NT
    TILE2, TILE3 = NT, 2 * NT

    x_rows = x.rearrange("(q t a) d -> q a t d", q=G, a=B)
    out_rows = out.rearrange("(q t a) d -> q a t d", q=G, a=B)
    adj_src = adj.rearrange("(c t b) (q j) -> q t b c j", c=G, b=B, q=G)
    adj_half = adj.rearrange("(r k a) (q h m) -> h r k a q m", r=G, a=B, q=G, h=2)
    kept_half = adj_t_blocks.rearrange("(h t) p (k m) -> h k p t m", h=2, m=P)

    ctx = ExitStack()
    with ctx:
        def sb(name, shape, dt=fp32):
            return ctx.enter_context(nc.sbuf_tensor(name, shape, dt))

        def sem(name):
            return ctx.enter_context(nc.semaphore(name))

        act_hi = sb("act_hi", [P, NT, D], fp32r)
        act_lo = sb("act_lo", [P, NT, D], fp32r)
        nxt = sb("nxt", [P, NT, D])
        x_in = nxt[:, 4:8, :]
        res = sb("res", [P, NT, D])
        blk_hi = sb("blk_hi", [P, 2, N], fp32r)
        blk_lo = sb("blk_lo", [P, 2, N], fp32r)
        nat = sb("nat", [P, 2, N])
        tr = sb("tr", [P, 2, N])
        hT_hi = sb("hT_hi", [P, 2, D], fp32r)
        hT_lo = sb("hT_lo", [P, 2, D], fp32r)
        ident = sb("ident", [P, P])
        ident2 = sb("ident2", [P, P])
        same_row = sb("same_row", [P, G, P])
        row_buf = sb("row_buf", [P, D])
        row_part = sb("row_part", [P, NT, G])
        col_part = sb("col_part", [P, 2, NT])
        col_sum = sb("col_sum", [P, NT])
        dinv = sb("dinv", [P, NT])
        half_dinv = sb("half_dinv", [P, NT])
        deg = sb("deg", [P, NT])
        deg_pos = sb("deg_pos", [P, NT])
        deg_c = sb("deg_c", [P, NT])
        deg_t = sb("deg_t", [P, 4, NT])
        stats = sb("stats", [P, 2, 6])
        mv = sb("mv", [P, 2, 2])
        ln_t = sb("ln_t", [P, 4, 2])
        rstd = sb("rstd", [P, 2])
        shift = sb("shift", [P, 2])

        acc = ctx.enter_context(nc.psum_tensor("acc", [P, 8, D], fp32))
        HT, FIRST, SUM = 2, 2, 4

        w_raw, w_hi, w_lo = nat[:, 1, :], blk_hi[:, 1, :], blk_lo[:, 1, :]

        def unit(t, s):
            return t[:, s // 2, (s % 2) * (N // 2):(s % 2 + 1) * (N // 2)]

        s_x = [sem("s_x_in0"), sem("s_x_in1")]
        s_w = sem("s_w_loaded")
        s_bias = sem("s_bias_loaded")
        s_ident = sem("s_ident")
        s_same = sem("s_same_row")
        s_whi = sem("s_w_hi")
        s_wlo = sem("s_w_lo")
        s_xb = sem("s_x_plus_bias")
        s_var = sem("s_var_ready")
        s_root = sem("s_root_ready")
        s_norm = sem("s_norm_ready")
        s_h = sem("s_h_ready")
        s_hT = sem("s_hT_psum")
        s_hThi = sem("s_hT_hi")
        s_hTlo = sem("s_hT_lo")
        s_sup = sem("s_support_psum")
        s_ahi = sem("s_act_hi")
        s_alo = sem("s_act_lo")
        s_nat = [sem("s_nat0"), sem("s_nat1")]
        s_natu = [sem(f"s_nat_unit{s}") for s in range(S)]
        s_tru = [sem(f"s_tr_unit{s}") for s in range(S)]
        s_tr = [sem("s_tr0"), sem("s_tr1")]
        s_keep = [sem("s_keep0"), sem("s_keep1")]
        s_trn = sem("s_transposed")
        s_rsum = sem("s_row_part")
        s_cinit = sem("s_col_init")
        s_csum = sem("s_col_sum")
        s_rtot = sem("s_row_sums_psum")
        s_sadd = sem("s_sum_added")
        s_sym = sem("s_sym")
        s_bhi = sem("s_blk_hi")
        s_blo = sem("s_blk_lo")
        s_used = sem("s_act_used")
        s_unit = sem("s_unit_done")
        s_acc = sem("s_acc_done")
        s_x1 = sem("s_x1")
        s_res = sem("s_res")
        s_h1 = sem("s_h1")
        s_z = sem("s_z")
        s_o = sem("s_o")
        s_dvar = sem("s_deg_ready")
        s_droot = sem("s_deg_root")
        s_dinv = sem("s_dinv")
        s_ch = sem("s_dve_chain")
        s_out = sem("s_out")

        block = ctx.enter_context(nc.Block())

        @block.sync
        def _(sp):
            def group(q):
                return slice(B * q, B * (q + 1))

            def load_x(j, par):
                for q in range(G):
                    sp.dma_start(x_in[group(q), 2 * par:2 * par + 2, :], x_rows[q, :, bass.ds(2 * j, 2), :])\
                      .then_inc(s_x[par], 16)

            def reload_x(j, par):
                sp.wait_ge(s_h, 2 * j - 2)
                sp.wait_ge(s_xb, 2 * j - 2)
                load_x(j, par)

            def load_src(t, par):
                for q in range(G):
                    sp.dma_start(nat[group(q), par, :].rearrange("b (c j) -> b c j", c=G), adj_src[q, t, :, :, :])\
                      .then_inc(s_nat[par], 16)

            load_x(0, 0)
            for c in range(ND):
                sp.dma_start(w_raw[:, c * D:(c + 1) * D], weight[c * P:(c + 1) * P, :]).then_inc(s_w, 16)
            load_x(1, 1)
            sp.dma_start(row_buf[:, :], bias.rearrange("(a n) -> a n", a=1).broadcast_to([P, D])).then_inc(s_bias, 16)
            load_src(0, 0)
            with sp.Fori(1, NT // 4) as i:
                reload_x(2 * i, 0)
                reload_x(2 * i + 1, 1)
            sp.wait_ge(s_whi, 1)
            sp.wait_ge(s_wlo, 1)
            load_src(1, 1)

            def keep(t, par):
                sp.wait_ge(s_trn, t + 1)
                sp.dma_start(adj_t_blocks[t, :, :], tr[:, par, :]).then_inc(s_keep[par], 16)

            def layer1(t, par):
                keep(t, par)
                sp.wait_ge(s_rsum, t + 1)
                load_src(t + 2, par)

            with sp.Fori(0, NT // 2 - 1) as i:
                layer1(2 * i, 0)
                layer1(2 * i + 1, 1)
            keep(NT - 2, 0)
            keep(NT - 1, 1)

            def load_unit(half, k, s):
                for q in range(G):
                    sp.dma_start(unit(nat, s)[group(q), :].rearrange("a (q m) -> a q m", q=G),
                                 adj_half[half, q, k, :, :, :]).then_inc(s_natu[s], 16)
                sp.dma_start(unit(tr, s).rearrange("p (t m) -> p t m", m=P), kept_half[half, k, :, :, :])\
                  .then_inc(s_tru[s], 16)

            for s in range(S):
                par = s // 2
                sp.wait_ge(s_rsum, NT - 1 + par)
                sp.wait_ge(s_keep[par], 16 * (NT // 2))
                sp.wait_ge(s_keep[1], 16 * (H // 2))
                sp.wait_ge(s_blo, NT - 1 + par)
                load_unit(0, s, s)

            def reload_unit(half, k, s):
                sp.wait_ge(s_sym, NT * half + k - S + 1)
                sp.nop(nofuse=True)
                sp.wait_ge(s_blo, SPLIT2 + NT * half + k - S + 1)
                load_unit(half, k, s)

            with sp.Fori(1, NT // S) as i:
                for s in range(S):
                    reload_unit(0, S * i + s, s)
            with sp.Fori(0, NT // S) as i:
                for s in range(S):
                    reload_unit(1, S * i + s, s)

            def load_kept(v, par):
                sp.dma_start(tr[:, par, :], adj_t_blocks[v, :, :]).then_inc(s_tr[par], 16)

            sp.wait_ge(s_blo, SPLIT3 - 2)
            load_kept(0, 0)
            sp.wait_ge(s_blo, SPLIT3)
            load_kept(1, 1)

            def reload_kept(v, par):
                sp.wait_ge(s_blo, SPLIT3 + v - 1)
                load_kept(v, par)

            def store(v):
                sp.wait_ge(s_o, v + 1)
                for q in range(G):
                    sp.dma_start(out_rows[q, :, v, :], res[group(q), v, :]).then_inc(s_out, 16)

            reload_kept(2, 0)
            with sp.Fori(0, NT // 2 - 2) as i:
                reload_kept(2 * i + 3, 1)
                store(2 * i)
                reload_kept(2 * i + 4, 0)
                store(2 * i + 1)
            reload_kept(NT - 1, 1)
            with sp.Fori(NT - 4, NT) as v:
                store(v)
            sp.wait_ge(s_out, 16 * G * NT)

        @block.gpsimd
        def _(pool):
            nc.gpsimd.memset(ident[:, :], 0.0).then_inc(s_ident, 1)
            nc.gpsimd.memset(ident2[:, :], 0.0).then_inc(s_ident, 1)
            pool.wait_ge(s_ident, 2)
            for m, v in ((ident, 1.0), (ident2, 2.0)):
                nc.gpsimd.affine_select(out=m[:, :], in_=m[:, :], compare_op=ALU.not_equal, fill=v,
                                        base=0, pattern=[[-1, P]], channel_multiplier=1).then_inc(s_ident, 1)

            def add_bias(t, slot, j):
                pool.wait_ge(s_x[slot // 2], 16 * G * (j + 1))
                nc.gpsimd.tensor_tensor(res[:, t, :], x_in[:, slot, :], row_buf[:, :], ALU.add).then_inc(s_xb, 1)

            pool.wait_ge(s_bias, 16)
            with pool.Fori(0, NT // 4) as i:
                for slot in range(4):
                    add_bias(4 * i + slot, slot, i)

            nc.gpsimd.memset(col_sum[:, :], 0.0).then_inc(s_cinit, 1)
            nc.gpsimd.memset(same_row[:, :, :], 0.0).then_inc(s_same, 1)
            pool.wait_ge(s_same, 1)
            for c in range(G):
                for q in range(G):
                    part = same_row[:, c, B * c:B * (c + 1)]
                    nc.gpsimd.affine_select(out=part, in_=part, compare_op=ALU.not_equal, fill=1.0, base=-B * q,
                                            pattern=[[-1, B]], channel_multiplier=1).then_inc(s_same, 1)
                    pool.wait_ge(s_same, 2 + G * c + q)

            def add_cols(t, par):
                pool.wait_ge(s_bhi, t + 1)
                nc.gpsimd.tensor_tensor(col_sum[:, :], col_sum[:, :], col_part[:, par, :], ALU.add)\
                  .then_inc(s_csum, 1)
                pool.wait_ge(s_csum, t + 1)

            def copy_x1(t):
                pool.wait_ge(s_x1, t + 1)
                nc.gpsimd.tensor_copy(res[:, t, :], row_buf[:, :]).then_inc(s_res, 1)

            pool.wait_ge(s_cinit, 1)
            add_cols(0, 0)
            add_cols(1, 1)
            with pool.Fori(0, NT // 2 - 1) as i:
                copy_x1(2 * i)
                add_cols(2 * i + 2, 0)
                copy_x1(2 * i + 1)
                add_cols(2 * i + 3, 1)
            copy_x1(NT - 2)
            copy_x1(NT - 1)

        @block.tensor
        def _(pe):
            def product(dst, w, a, first, last):
                nc.tensor.matmul(dst, w[0], a[0], start=first, stop=False)
                nc.tensor.matmul(dst, w[0], a[1], start=False, stop=False)
                return nc.tensor.matmul(dst, w[1], a[0], start=False, stop=last)

            def transpose_h(t, par, reused=True):
                pe.wait_ge(s_h, t + 1)
                if reused:
                    pe.wait_ge(s_hTlo, t - 1)
                for c in range(ND):
                    ins = nc.tensor.transpose(acc[:, HT + par, c * P:(c + 1) * P],
                                              nxt[:, par, c * P:(c + 1) * P], ident[:, :])
                ins.then_inc(s_hT, 1)

            def support(t, par, reused=True):
                pe.wait_ge(s_hThi, t + 1)
                pe.wait_ge(s_hTlo, t + 1)
                if reused:
                    pe.wait_ge(s_alo, t - 1)
                for c in range(ND):
                    k, n = slice(c * P, (c + 1) * P), slice(c * D, (c + 1) * D)
                    ins = product(acc[:, par, :], (hT_hi[:, par, k], hT_lo[:, par, k]),
                                  (w_hi[:, n], w_lo[:, n]), c == 0, c == ND - 1)
                ins.then_inc(s_sup, 1)

            def act_tile(k):
                return act_hi[:, k, :], act_lo[:, k, :]

            def aggregate(split, bank, par, fresh=None, release=False):
                pe.wait_ge(s_bhi, split)
                pe.wait_ge(s_blo, split)
                for k in range(NT):
                    if fresh is not None:
                        pe.wait_ge(s_ahi, fresh + k + 1)
                        pe.wait_ge(s_alo, fresh + k + 1)
                    m = slice(k * P, (k + 1) * P)
                    ins = product(acc[:, bank, :], (blk_hi[:, par, m], blk_lo[:, par, m]), act_tile(k),
                                  k == 0, k == NT - 1)
                    if release and k < NT - 1:
                        ins.then_inc(s_used, 1)
                ins.then_inc(s_acc, 1)

            pe.wait_ge(s_ident, 4)
            transpose_h(0, 0, False)
            transpose_h(1, 1, False)
            pe.wait_ge(s_whi, 1)
            pe.wait_ge(s_wlo, 1)
            support(0, 0, False)
            transpose_h(2, 0)
            support(1, 1, False)
            with pe.Fori(0, NT // 2 - 2) as i:
                transpose_h(2 * i + 3, 1)
                support(2 * i + 2, 0)
                transpose_h(2 * i + 4, 0)
                support(2 * i + 3, 1)
            transpose_h(NT - 1, 1)
            support(NT - 2, 0)
            support(NT - 1, 1)

            pe.wait_ge(s_alo, NT - 1)
            aggregate(1, 0, 0, fresh=0)
            aggregate(2, 1, 1)

            def layer1(t, par):
                pe.wait_ge(s_x1, t - 1)
                aggregate(t + 1, par, par)

            with pe.Fori(1, NT // 2 - 1) as i:
                layer1(2 * i, 0)
                layer1(2 * i + 1, 1)
            layer1(NT - 2, 0)
            pe.wait_ge(s_same, 1 + G * G)
            pe.wait_ge(s_rsum, NT)
            for c in range(G):
                ins = nc.tensor.matmul(acc[:, SUM, 0:NT], same_row[:, c, :], row_part[:, :, c],
                                       start=c == 0, stop=c == G - 1)
            ins.then_inc(s_rtot, 1)
            pe.wait_ge(s_x1, NT - 2)
            aggregate(NT, 1, 1, release=True)

            def unit_products(half, k, s, bank_free=None, done=None):
                u = NT * half + k
                pe.wait_ge(s_bhi, SPLIT2 + u + 1)
                pe.wait_ge(s_blo, SPLIT2 + u + 1)
                if half == 0:
                    pe.wait_ge(s_ahi, NT + k + 1)
                    pe.wait_ge(s_alo, NT + k + 1)
                for i in range(H):
                    if bank_free is not None:
                        bank_free(i)
                    m = slice(i * P, (i + 1) * P)
                    ins = product(acc[:, (FIRST + i) % 8, :], (unit(blk_hi, s)[:, m], unit(blk_lo, s)[:, m]),
                                  act_tile(k), bank_free is not None, done is not None)
                    if done is not None:
                        ins.then_inc(done, 1)
                if done is None:
                    ins.then_inc(s_unit, 1)

            def free_first(i):
                if (FIRST + i) % 8 == SUM:
                    pe.wait_ge(s_dvar, 1)
                if (FIRST + i) % 8 == 0:
                    pe.wait_ge(s_x1, NT - 1)
                if (FIRST + i) % 8 == 1:
                    pe.wait_ge(s_x1, NT)

            def free_second(i):
                pe.wait_ge(s_z, i + 1)

            for half, bank_free in ((0, free_first), (1, free_second)):
                unit_products(half, 0, 0, bank_free=bank_free)
                with pe.Fori(0, NT // S - 1) as i:
                    for s in range(S):
                        unit_products(half, S * i + s + 1, (s + 1) % S)
                unit_products(half, NT - 3, 1)
                unit_products(half, NT - 2, 2)
                unit_products(half, NT - 1, 3, done=s_acc)

            pe.wait_ge(s_z, H + 1)
            aggregate(SPLIT3 + 1, FIRST, 0, fresh=2 * NT)
            aggregate(SPLIT3 + 2, FIRST + 1, 1)
            with pe.Fori(1, NT // 2) as i:
                pe.wait_ge(s_o, 2 * i - 1)
                aggregate(SPLIT3 + 2 * i + 1, FIRST, 0)
                pe.wait_ge(s_o, 2 * i)
                aggregate(SPLIT3 + 2 * i + 2, FIRST + 1, 1)

        @block.scalar
        def _(act):
            def root(n, cols):
                act.wait_ge(s_var, n + 1)
                nc.scalar.activation(ln_t[:, 1, 0:cols], ln_t[:, 0, 0:cols], ACT.Sqrt).then_inc(s_root, 1)

            def normalize(t, slot, pair, reused=True):
                par = slot % 2
                act.wait_ge(s_norm, pair + 1)
                if reused:
                    act.wait_ge(s_hT, t - 1)
                nc.scalar.activation(nxt[:, par, :], x_in[:, slot, :], ACT.Relu, scale=rstd[:, par:par + 1],
                                     bias=shift[:, par:par + 1]).then_inc(s_h, 1)

            def split_hT(t, par, reused=True):
                act.wait_ge(s_hT, t + 1)
                if reused:
                    act.wait_ge(s_sup, t - 1)
                nc.scalar.copy(hT_hi[:, par, :], acc[:, HT + par, :]).then_inc(s_hThi, 1)

            def split_support(t, par):
                act.wait_ge(s_sup, t + 1)
                nc.scalar.copy(act_hi[:, t, :], acc[:, par, :]).then_inc(s_ahi, 1)

            def split_rows(t, par, used=None, blocks=(0, NT)):
                act.wait_ge(s_trn, t + 1)
                if used is not None:
                    act.wait_ge(s_acc, used)
                    act.wait_ge(s_csum, t - 1)
                for k in range(*blocks):
                    m = slice(k * P, (k + 1) * P)
                    ins = nc.scalar.activation(blk_hi[:, par, m], tr[:, par, m], ACT.Copy,
                                               accum_out=col_part[:, par, k:k + 1])
                if blocks[1] == NT:
                    ins.then_inc(s_bhi, 1)

            def normalize1(t):
                act.wait_ge(s_norm, NT // 2 + t + 1)
                nc.scalar.activation(nxt[:, t, :], row_buf[:, :], ACT.Relu, scale=rstd[:, 0:1],
                                     bias=shift[:, 0:1]).then_inc(s_h1, 1)

            def root1(t):
                root(NT // 2 + t, 1)

            root(0, 2)
            normalize(0, 0, 0, False)
            normalize(1, 1, 0, False)
            act.wait_ge(s_w, 16 * ND)
            nc.scalar.copy(w_hi, w_raw).then_inc(s_whi, 1)
            split_hT(0, 0, False)
            root(1, 2)

            def prepare(i, pair, norm, roots):
                if norm:
                    normalize(2 * i + 2, 2 * pair, i + 1)
                split_hT(2 * i + 1, 1, not isinstance(i, int) or i > 0)
                split_support(2 * i, 0)
                if norm:
                    normalize(2 * i + 3, 2 * pair + 1, i + 1)
                split_hT(2 * i + 2, 0)
                if roots:
                    root(i + 2, 2)

            prepare(0, 1, True, True)
            split_support(1, 1)
            with act.Fori(0, NT // 4 - 2) as i:
                prepare(2 * i + 1, 0, True, True)
                split_support(4 * i + 3, 1)
                prepare(2 * i + 2, 1, True, True)
                split_support(4 * i + 5, 1)
            prepare(NT // 2 - 3, 0, True, True)
            split_support(NT - 5, 1)
            prepare(NT // 2 - 2, 1, True, False)
            split_support(NT - 3, 1)
            split_hT(NT - 1, 1)
            split_rows(0, 0, blocks=(0, NT // 2))
            split_support(NT - 2, 0)
            split_rows(0, 0, blocks=(NT // 2, NT))
            split_support(NT - 1, 1)

            act.wait_ge(s_sup, NT)
            split_rows(1, 1)
            split_rows(2, 0, 1)
            root1(0)
            normalize1(0)
            with act.Fori(1, NT // 2 - 1) as i:
                split_rows(2 * i + 1, 1, 2 * i)
                root1(2 * i - 1)
                normalize1(2 * i - 1)
                split_rows(2 * i + 2, 0, 2 * i + 1)
                root1(2 * i)
                normalize1(2 * i)
            split_rows(NT - 1, 1, NT - 2)
            root1(NT - 3)
            normalize1(NT - 3)

            def split_unit(u, s, used):
                act.wait_ge(s_sym, u + 1)
                act.wait_ge(*used)
                nc.scalar.copy(unit(blk_hi, s), unit(tr, s)).then_inc(s_bhi, 1)

            def split_g(k, used=None):
                if used is not None:
                    act.wait_ge(s_used, used)
                act.wait_ge(s_h1, k + 1)
                nc.scalar.activation(act_hi[:, k, :], nxt[:, k, :], ACT.Copy, scale=dinv[:, bass.ds(k, 1)])\
                  .then_inc(s_ahi, 1)

            root1(NT - 2)
            act.wait_ge(s_dvar, 1)
            nc.scalar.activation(deg_t[:, 0, :], deg_c[:, :], ACT.Sqrt).then_inc(s_droot, 1)
            split_unit(0, 0, (s_acc, NT - 1))
            normalize1(NT - 2)
            act.wait_ge(s_dinv, 1)
            split_g(0, 1)
            split_unit(1, 1, (s_acc, NT - 1))
            split_g(1, 2)
            root1(NT - 1)
            split_unit(2, 2, (s_acc, NT))
            normalize1(NT - 1)
            split_g(2)
            split_unit(3, 3, (s_acc, NT))
            split_g(3)
            with act.Fori(1, NT // S) as i:
                for s in range(S):
                    split_unit(S * i + s, s, (s_unit, S * i + s - S + 1))
                    split_g(S * i + s)

            def take_z(u, bank):
                act.wait_ge(s_acc, TILE2 + u + 1)
                nc.scalar.activation(nxt[:, u, :], acc[:, bank % 8, :], ACT.Copy,
                                     scale=half_dinv[:, bass.ds(u, 1)]).then_inc(s_z, 1)

            for s in range(S - 1):
                split_unit(NT + s, s, (s_unit, NT - S + s + 1))
            act.wait_ge(s_alo, 2 * NT)
            for t in range(H):
                take_z(t, FIRST + t)
            split_unit(NT + S - 1, S - 1, (s_acc, NT + H))
            with act.Fori(1, NT // S) as i:
                for s in range(S):
                    split_unit(NT + S * i + s, s, (s_unit, NT + S * i + s - S))

            def split_z(k):
                act.wait_ge(s_z, k + 1)
                nc.scalar.copy(act_hi[:, k, :], nxt[:, k, :]).then_inc(s_ahi, 1)

            def split_kept(v, par, loads, used):
                act.wait_ge(s_tr[par], 16 * loads)
                act.wait_ge(*used)
                nc.scalar.copy(blk_hi[:, par, :], tr[:, par, :]).then_inc(s_bhi, 1)

            with act.Fori(0, H) as k:
                act.wait_ge(s_unit, NT + k)
                split_z(k)
            split_kept(0, 0, 1, (s_unit, 2 * NT - 3))
            for k in range(H, NT):
                take_z(k, FIRST + k - H)
                if k < NT - 1:
                    act.wait_ge(s_unit, NT + k)
                split_z(k)
            split_kept(1, 1, 1, (s_acc, TILE3))

            with act.Fori(1, NT // 2) as i:
                split_kept(2 * i, 0, i + 1, (s_acc, TILE3 + 2 * i - 1))
                split_kept(2 * i + 1, 1, i + 1, (s_acc, TILE3 + 2 * i))

        @block.vector
        def _(dve):
            STATS, NORM = 2, 4
            PAIR = 2 * STATS + NORM
            TILE = STATS + NORM
            BASE1 = (NT // 2) * PAIR

            def chained(ins, n):
                ins.then_inc(s_ch, 1)
                dve.wait_ge(s_ch, n)

            def tile_stats(tile, col, n):
                dve.nop(nofuse=True)
                chained(nc.vector.bn_stats(stats[:, col, :], tile), n + 1)
                dve.nop(nofuse=True)
                chained(nc.vector.bn_aggr(mv[:, col, :], stats[:, col, :]), n + 2)

            def variance(cols):
                nc.vector.tensor_scalar(ln_t[:, 0, 0:cols], mv[:, 0:cols, 1], EPS, None, ALU.add)\
                  .then_inc(s_var, 1)

            def inv_root(out_, v, r, a, b, n):
                chained(nc.vector.reciprocal(r, r), n + 1)
                chained(nc.vector.tensor_tensor(a, r, r, ALU.mult), n + 2)
                chained(nc.vector.scalar_tensor_tensor(b, a, -0.5, v, ALU.mult, ALU.mult), n + 3)
                chained(nc.vector.scalar_tensor_tensor(out_, b, 1.5, r, ALU.add, ALU.mult), n + 4)

            def norm(step, cols, n):
                dve.wait_ge(s_root, step + 1)
                inv_root(rstd[:, 0:cols], ln_t[:, 0, 0:cols], ln_t[:, 1, 0:cols], ln_t[:, 2, 0:cols],
                         ln_t[:, 3, 0:cols], n)
                nc.vector.scalar_tensor_tensor(shift[:, 0:cols], mv[:, 0:cols, 0], -1.0, rstd[:, 0:cols],
                                               ALU.mult, ALU.mult).then_inc(s_norm, 1)

            def split_hT(t, par):
                dve.wait_ge(s_hThi, t + 1)
                nc.vector.tensor_tensor(hT_lo[:, par, :], acc[:, HT + par, :], hT_hi[:, par, :].bitcast(fp32),
                                        ALU.subtract).then_inc(s_hTlo, 1)

            def split_support(t, par):
                dve.wait_ge(s_ahi, t + 1)
                nc.vector.tensor_tensor(act_lo[:, t, :], acc[:, par, :], act_hi[:, t, :].bitcast(fp32),
                                        ALU.subtract).then_inc(s_alo, 1)

            def transpose_rows(t, par, j):
                dve.wait_ge(s_nat[par], 16 * G * (j + 1))
                if not isinstance(t, int) or t > 1:
                    dve.wait_ge(s_keep[par], 16 * j)
                    dve.wait_ge(s_blo, t - 1)
                nc.vector.transpose(tr[:, par, :].rearrange("p (k c b) -> p c k b", c=G, b=B),
                                    nat[:, par, :].rearrange("p (c k a) -> p c k a", c=G, a=B))\
                  .then_inc(s_trn, 1)

            def sum_rows(t, par):
                nc.vector.tensor_reduce(row_part[:, t, :], nat[:, par, :].rearrange("p (c j) -> p c j", c=G),
                                        AX.X, ALU.add).then_inc(s_rsum, 1)

            def split_block(n, hi, lo, raw):
                dve.wait_ge(s_bhi, n + 1)
                nc.vector.tensor_tensor(lo, raw, hi.bitcast(fp32), ALU.subtract).then_inc(s_blo, 1)

            def split_tile(n, par):
                split_block(n, blk_hi[:, par, :], blk_lo[:, par, :], tr[:, par, :])

            def take_x1(t, par, n):
                dve.wait_ge(s_acc, t + 1)
                if not isinstance(t, int) or t > 0:
                    dve.wait_ge(s_h1, t)
                    dve.wait_ge(s_res, t)
                nc.vector.tensor_tensor(row_buf[:, :], acc[:, par, :], res[:, t, :], ALU.add).then_inc(s_x1, 1)
                dve.wait_ge(s_x1, t + 1)
                tile_stats(row_buf[:, :], 0, n)
                variance(1)

            def norm1(t, n):
                norm(NT // 2 + t, 1, n)

            for j in range(2):
                dve.wait_ge(s_x[j], 16 * G)
                tile_stats(x_in[:, 2 * j, :], 0, PAIR * j)
                tile_stats(x_in[:, 2 * j + 1, :], 1, PAIR * j + STATS)
                variance(2)
                if j == 1:
                    dve.wait_ge(s_whi, 1)
                    nc.vector.tensor_tensor(w_lo, w_raw, w_hi.bitcast(fp32), ALU.subtract).then_inc(s_wlo, 1)
                    split_hT(0, 0)
                norm(j, 2, PAIR * j + 2 * STATS)

            def prepare(i, par, j):
                dve.wait_ge(s_x[par], 16 * G * (j + 1))
                tile_stats(x_in[:, 2 * par, :], 0, PAIR * (i + 2))
                split_hT(2 * i + 1, 1)
                split_support(2 * i, 0)
                tile_stats(x_in[:, 2 * par + 1, :], 1, PAIR * (i + 2) + STATS)
                variance(2)
                split_hT(2 * i + 2, 0)
                split_support(2 * i + 1, 1)
                norm(i + 2, 2, PAIR * (i + 2) + 2 * STATS)

            with dve.Fori(0, NT // 4 - 1) as i:
                prepare(2 * i, 0, i + 1)
                prepare(2 * i + 1, 1, i + 1)
            split_hT(NT - 3, 1)
            split_support(NT - 4, 0)
            split_hT(NT - 2, 0)
            transpose_rows(0, 0, 0)
            split_support(NT - 3, 1)
            split_hT(NT - 1, 1)
            sum_rows(0, 0)
            split_support(NT - 2, 0)
            transpose_rows(1, 1, 0)
            split_support(NT - 1, 1)

            dve.wait_ge(s_xb, NT)
            split_tile(0, 0)
            sum_rows(1, 1)
            transpose_rows(2, 0, 1)
            sum_rows(2, 0)
            split_tile(1, 1)

            def layer1(t, par, j, n):
                take_x1(t - 1, 1 - par, n)
                transpose_rows(t + 2, par, j + 1)
                sum_rows(t + 2, par)
                norm1(t - 1, n + STATS)
                split_tile(t + 1, 1 - par)

            layer1(1, 1, 0, BASE1)
            with dve.Fori(1, NT // 2 - 1) as i:
                layer1(2 * i, 0, i, BASE1 + TILE * (2 * i - 1))
                layer1(2 * i + 1, 1, i, BASE1 + TILE * (2 * i))
            n = BASE1 + TILE * (NT - 3)
            take_x1(NT - 3, 1, n)
            norm1(NT - 3, n + STATS)
            split_tile(NT - 1, 1)

            def symmetric(half, s, loads, diag=None):
                dve.wait_ge(s_natu[s], 16 * G * loads)
                dve.wait_ge(s_tru[s], 16 * loads)
                blocks = unit(tr, s).rearrange("p (t q b) -> p t q b", q=G, b=B)
                ins = nc.vector.tensor_tensor(blocks, blocks,
                                              unit(nat, s).rearrange("p (q t b) -> p t q b", q=G, b=B), ALU.add)
                if diag is None:
                    ins.then_inc(s_sym, 1)
                else:
                    ins.then_inc(s_sadd, 1)
                    dve.wait_ge(s_sadd, diag + 1 + H * half)
                    own = unit(tr, s)[:, bass.ds(P * diag, P)]
                    nc.vector.tensor_tensor(own, own, ident2[:, :], ALU.add).then_inc(s_sym, 1)

            def split_unit(u, s):
                split_block(SPLIT2 + u, unit(blk_hi, s), unit(blk_lo, s), unit(tr, s))

            def split_g(k):
                dve.wait_ge(s_ahi, NT + k + 1)
                nc.vector.scalar_tensor_tensor(act_lo[:, k, :], nxt[:, k, :], dinv[:, bass.ds(k, 1)],
                                               act_hi[:, k, :].bitcast(fp32), ALU.mult, ALU.subtract)\
                  .then_inc(s_alo, 1)

            n = BASE1 + TILE * (NT - 2)
            take_x1(NT - 2, 0, n)
            dve.wait_ge(s_csum, NT)
            dve.wait_ge(s_rtot, 1)
            chained(nc.vector.tensor_tensor(deg[:, :], acc[:, SUM, 0:NT], col_sum[:, :], ALU.add), n + STATS + 1)
            chained(nc.vector.tensor_scalar(deg[:, :], deg[:, :], 0.5, 1.0, ALU.mult, ALU.add), n + STATS + 2)
            chained(nc.vector.tensor_scalar(deg_pos[:, :], deg[:, :], 0.0, None, ALU.is_gt), n + STATS + 3)
            nc.vector.tensor_scalar(deg_c[:, :], deg[:, :], 2.0 ** -100, None, ALU.max).then_inc(s_dvar, 1)
            n += STATS + 3
            symmetric(0, 0, 1, 0)
            dve.wait_ge(s_droot, 1)
            inv_root(deg_t[:, 1, :], deg_c[:, :], deg_t[:, 0, :], deg_t[:, 2, :], deg_t[:, 3, :], n)
            chained(nc.vector.tensor_tensor(dinv[:, :], deg_t[:, 1, :], deg_pos[:, :], ALU.mult), n + 5)
            nc.vector.tensor_scalar(half_dinv[:, :], dinv[:, :], 0.5, None, ALU.mult).then_inc(s_dinv, 1)
            norm1(NT - 2, n + 5)
            n += 5 + NORM
            symmetric(0, 1, 1, 1)
            split_unit(0, 0)
            split_g(0)
            split_unit(1, 1)
            split_g(1)
            symmetric(0, 2, 1, 2)
            take_x1(NT - 1, 1, n)
            symmetric(0, 3, 1, 3)
            norm1(NT - 1, n + STATS)
            split_unit(2, 2)
            split_g(2)
            split_unit(3, 3)
            split_g(3)

            def units(half, j, diag):
                u, loads = NT * half + S * j, NT // S * half + j + 1
                own = [S * j + s - (H if half else 0) if diag else None for s in range(S)]
                symmetric(half, 0, loads, own[0])
                for s in range(S):
                    if s < S - 1:
                        symmetric(half, s + 1, loads, own[s + 1])
                    split_unit(u + s, s)
                    if half == 0:
                        split_g(S * j + s)

            units(0, 1, True)
            with dve.Fori(H // S, NT // S) as i:
                units(0, i, False)
            with dve.Fori(0, H // S) as i:
                units(1, i, False)
            with dve.Fori(H // S, NT // S) as i:
                units(1, i, True)

            def split_z(k):
                dve.wait_ge(s_ahi, 2 * NT + k + 1)
                nc.vector.tensor_tensor(act_lo[:, k, :], nxt[:, k, :], act_hi[:, k, :].bitcast(fp32),
                                        ALU.subtract).then_inc(s_alo, 1)

            with dve.Fori(0, H) as k:
                split_z(k)
            split_tile(SPLIT3, 0)
            with dve.Fori(H, NT) as k:
                split_z(k)
            split_tile(SPLIT3 + 1, 1)

            def take_out(v, bank):
                dve.wait_ge(s_acc, TILE3 + v + 1)
                nc.vector.tensor_tensor(res[:, v, :], acc[:, bank, :], res[:, v, :], ALU.add).then_inc(s_o, 1)

            dve.wait_ge(s_res, NT)
            with dve.Fori(1, NT // 2) as i:
                take_out(2 * i - 2, FIRST)
                split_tile(SPLIT3 + 2 * i, 0)
                take_out(2 * i - 1, FIRST + 1)
                split_tile(SPLIT3 + 2 * i + 1, 1)
            take_out(NT - 2, FIRST)
            take_out(NT - 1, FIRST + 1)


_INS = ['x', 'adj', 'L0_gnn_weight', 'L0_gnn_bias']


def kernel(**inputs):
    import numpy as _np
    import concourse.bacc as _bacc
    from concourse import mybir as _mybir
    from concourse.bass_utils import run_bass_kernel_spmd as _run

    nc = _bacc.Bacc("TRN2", target_bir_lowering=False, num_devices=1)
    arrays, args = {}, []
    for name in _INS:
        a = _np.ascontiguousarray(inputs[name])
        arrays[f"in_{name}_dram"] = a
        args.append(nc.dram_tensor(f"in_{name}_dram", a.shape, _mybir.dt.from_np(a.dtype), kind="ExternalInput").ap())
    shape = inputs['x'].shape
    rows = inputs['adj'].shape[0]
    kept = nc.dram_tensor("adj_t_blocks", (rows // 128, 128, rows), _mybir.dt.float32, kind="Internal").ap()
    result = nc.dram_tensor("out_dram", shape, _mybir.dt.float32, kind="ExternalOutput").ap()
    two_layer_graph_conv(nc, *args, kept, result)
    r = _run(nc, [arrays], core_ids=[0])
    return r.results[0]["out_dram"]
```

```python
import concourse.bass as bass
from concourse import mybir
from contextlib import ExitStack


def two_layer_graph_conv(nc, x, adj, weight, bias, adj_t_blocks, out):
    fp32 = mybir.dt.float32
    fp32r = mybir.dt.float32r
    ALU = mybir.AluOpType
    ACT = mybir.ActivationFunctionType

    P = 128
    B = 32
    G = P // B
    N, D = x.shape
    NT = N // P
    ND = D // P
    W = N // G
    H = NT // 2
    S = 4
    EPS = 1e-5
    WARM_UP = 17
    HEAD_BLOCKS = 10
    SPLIT2, SPLIT3 = NT, NT + 2 * NT
    TILE2, TILE3 = NT, 2 * NT

    x_rows = x.rearrange("(q t a) d -> q a t d", q=G, a=B)
    out_rows = out.rearrange("(q t a) d -> q a t d", q=G, a=B)
    adj_src = adj.rearrange("(c t b) (q j) -> q t b c j", c=G, b=B, q=G)
    adj_half = adj.rearrange("(r k a) (q h m) -> h r k a q m", r=G, a=B, q=G, h=2)
    kept_half = adj_t_blocks.rearrange("(h t) p (k m) -> h k p t m", h=2, m=P)

    ctx = ExitStack()
    with ctx:
        def sb(name, shape, dt=fp32):
            return ctx.enter_context(nc.sbuf_tensor(name, shape, dt))

        def sem(name):
            return ctx.enter_context(nc.semaphore(name))

        act_hi = sb("act_hi", [P, NT, D], fp32r)
        act_lo = sb("act_lo", [P, NT, D], fp32r)
        nxt = sb("nxt", [P, NT, D])
        XS = 3
        x_in = nxt[:, 2:2 + 2 * XS, :]
        res = sb("res", [P, NT, D])
        blk_hi = sb("blk_hi", [P, 2, N], fp32r)
        blk_lo = sb("blk_lo", [P, 2, N], fp32r)
        nat = sb("nat", [P, 2, N])
        tr = sb("tr", [P, 2, N])
        hT_hi = sb("hT_hi", [P, 2, D], fp32r)
        hT_lo = sb("hT_lo", [P, 2, D], fp32r)
        ident = sb("ident", [P, P])
        ident2 = sb("ident2", [P, P])
        same_row = sb("same_row", [P, G, P])
        row_buf = sb("row_buf", [P, D])
        row_part = sb("row_part", [P, NT, G])
        col_part = sb("col_part", [P, 2, NT])
        col_sum = sb("col_sum", [P, NT])
        dinv = sb("dinv", [P, NT])
        half_dinv = sb("half_dinv", [P, NT])
        deg = sb("deg", [P, NT])
        deg_pos = sb("deg_pos", [P, NT])
        deg_c = sb("deg_c", [P, NT])
        deg_t = sb("deg_t", [P, 4, NT])
        stats = sb("stats", [P, 2, 6])
        mv = sb("mv", [P, 2, 2])
        ln_t = sb("ln_t", [P, 4, 2])
        rstd = sb("rstd", [P, 2])
        shift = sb("shift", [P, 2])

        acc = ctx.enter_context(nc.psum_tensor("acc", [P, 8, D], fp32))
        HT, FIRST, SUM, JUNK = 2, 2, 4, (4, 5, 6, 7)

        w_raw, w_hi, w_lo = nat[:, 1, :], blk_hi[:, 1, :], blk_lo[:, 1, :]

        def unit(t, s):
            return t[:, s // 2, (s % 2) * (N // 2):(s % 2 + 1) * (N // 2)]

        s_x_head = [sem("s_x_tile0"), sem("s_x_tile1")]
        s_x = [sem(f"s_x_in{j}") for j in range(XS)]
        s_w = [sem("s_w_loaded0"), sem("s_w_loaded1")]
        s_bias = sem("s_bias_loaded")
        s_ident = sem("s_ident")
        s_same = sem("s_same_row")
        s_whi = sem("s_w_hi")
        s_wlo = sem("s_w_lo")
        s_wlo2 = sem("s_w_lo2")
        s_xb = sem("s_x_plus_bias")
        s_var = sem("s_var_ready")
        s_root = sem("s_root_ready")
        s_norm = sem("s_norm_ready")
        s_h = sem("s_h_ready")
        s_hT = sem("s_hT_psum")
        s_hThi = sem("s_hT_hi")
        s_hTlo = sem("s_hT_lo")
        s_sup = sem("s_support_psum")
        s_ahi = sem("s_act_hi")
        s_alo = sem("s_act_lo")
        s_nat = [sem("s_nat0"), sem("s_nat1")]
        s_natu = [sem(f"s_nat_unit{s}") for s in range(S)]
        s_tru = [sem(f"s_tr_unit{s}") for s in range(S)]
        s_tr = [sem("s_tr0"), sem("s_tr1")]
        s_keep = [sem("s_keep0"), sem("s_keep1")]
        s_trn = sem("s_transposed")
        s_trn_half = sem("s_transposed_half")
        s_rsum = sem("s_row_part")
        s_cinit = sem("s_col_init")
        s_csum = sem("s_col_sum")
        s_rtot = sem("s_row_sums_psum")
        s_sadd = sem("s_sum_added")
        s_sym = sem("s_sym")
        s_hi_head = sem("s_blk_hi_head")
        s_lo_head = sem("s_blk_lo_head")
        s_bhi = sem("s_blk_hi")
        s_blo = sem("s_blk_lo")
        s_used = sem("s_act_used")
        s_unit = sem("s_unit_done")
        s_acc = sem("s_acc_done")
        s_x1 = sem("s_x1")
        s_res = sem("s_res")
        s_h1 = sem("s_h1")
        s_z = sem("s_z")
        s_o = sem("s_o")
        s_dvar = sem("s_deg_ready")
        s_droot = sem("s_deg_root")
        s_dinv = sem("s_dinv")
        s_ch = sem("s_dve_chain")
        s_out = sem("s_out")

        block = ctx.enter_context(nc.Block())

        @block.sync
        def _(sp):
            def group(q):
                return slice(B * q, B * (q + 1))

            def load_x(j, slot):
                for q in range(G):
                    sp.dma_start(x_in[group(q), 2 * slot:2 * slot + 2, :], x_rows[q, :, bass.ds(2 * j, 2), :])\
                      .then_inc(s_x[slot], 16)

            def reload_x(j, slot):
                sp.wait_ge(s_h, 2 * (j - XS) + 2)
                sp.wait_ge(s_xb, 2 * (j - XS) + 2)
                load_x(j, slot)

            def load_src(t, par):
                for q in range(G):
                    sp.dma_start(nat[group(q), par, :].rearrange("b (c j) -> b c j", c=G), adj_src[q, t, :, :, :])\
                      .then_inc(s_nat[par], 16)

            for t in range(2):
                for q in range(G):
                    sp.dma_start(x_in[group(q), t, :], x_rows[q, :, t, :]).then_inc(s_x_head[t], 16)
                if t == 0:
                    sp.dma_start(w_raw[:, 0:D], weight[0:P, :]).then_inc(s_w[0], 16)
            sp.dma_start(w_raw[:, D:].rearrange("p (c n) -> p c n", n=D),
                         weight[P:, :].rearrange("(c p) n -> p c n", p=P)).then_inc(s_w[1], 16)
            load_x(1, 1)
            load_x(2, 2)
            sp.dma_start(row_buf[:, :], bias.rearrange("(a n) -> a n", a=1).broadcast_to([P, D])).then_inc(s_bias, 16)
            reload_x(3, 0)
            reload_x(4, 1)
            load_src(0, 0)
            reload_x(5, 2)
            reload_x(6, 0)
            reload_x(7, 1)
            sp.wait_ge(s_wlo, ND - 1)
            sp.wait_ge(s_wlo2, 1)
            load_src(1, 1)

            def keep(t, par):
                sp.wait_ge(s_trn, t + 1)
                sp.dma_start(adj_t_blocks[t, :, :], tr[:, par, :]).then_inc(s_keep[par], 16)

            def layer1(t, par):
                keep(t, par)
                sp.wait_ge(s_rsum, t + 1)
                load_src(t + 2, par)

            with sp.Fori(0, NT // 2 - 1) as i:
                layer1(2 * i, 0)
                layer1(2 * i + 1, 1)
            keep(NT - 2, 0)
            keep(NT - 1, 1)

            def load_unit(half, k, s):
                for q in range(G):
                    sp.dma_start(unit(nat, s)[group(q), :].rearrange("a (q m) -> a q m", q=G),
                                 adj_half[half, q, k, :, :, :]).then_inc(s_natu[s], 16)
                sp.dma_start(unit(tr, s).rearrange("p (t m) -> p t m", m=P), kept_half[half, k, :, :, :])\
                  .then_inc(s_tru[s], 16)

            for s in range(S):
                par = s // 2
                sp.wait_ge(s_rsum, NT - 1 + par)
                sp.wait_ge(s_keep[par], 16 * (NT // 2))
                sp.wait_ge(s_keep[1], 16 * (H // 2))
                sp.wait_ge(s_blo, NT - 1 + par)
                load_unit(0, s, s)

            def reload_unit(half, k, s):
                sp.wait_ge(s_sym, NT * half + k - S + 1)
                sp.nop(nofuse=True)
                sp.wait_ge(s_blo, SPLIT2 + NT * half + k - S + 1)
                load_unit(half, k, s)

            with sp.Fori(1, NT // S) as i:
                for s in range(S):
                    reload_unit(0, S * i + s, s)
            with sp.Fori(0, NT // S) as i:
                for s in range(S):
                    reload_unit(1, S * i + s, s)

            def load_kept(v, par):
                sp.dma_start(tr[:, par, :], adj_t_blocks[v, :, :]).then_inc(s_tr[par], 16)

            sp.wait_ge(s_blo, SPLIT3 - 2)
            load_kept(0, 0)
            sp.wait_ge(s_blo, SPLIT3)
            load_kept(1, 1)

            def reload_kept(v, par):
                sp.wait_ge(s_blo, SPLIT3 + v - 1)
                load_kept(v, par)

            def store(v):
                sp.wait_ge(s_o, v + 1)
                for q in range(G):
                    sp.dma_start(out_rows[q, :, v, :], res[group(q), v, :]).then_inc(s_out, 16)

            reload_kept(2, 0)
            with sp.Fori(0, NT // 2 - 2) as i:
                reload_kept(2 * i + 3, 1)
                store(2 * i)
                reload_kept(2 * i + 4, 0)
                store(2 * i + 1)
            reload_kept(NT - 1, 1)
            with sp.Fori(NT - 4, NT) as v:
                store(v)
            sp.wait_ge(s_out, 16 * G * NT)

        @block.gpsimd
        def _(pool):
            nc.gpsimd.memset(ident[:, :], 0.0).then_inc(s_ident, 1)
            nc.gpsimd.memset(ident2[:, :], 0.0).then_inc(s_ident, 1)
            pool.wait_ge(s_ident, 2)
            for m, v in ((ident, 1.0), (ident2, 2.0)):
                nc.gpsimd.affine_select(out=m[:, :], in_=m[:, :], compare_op=ALU.not_equal, fill=v,
                                        base=0, pattern=[[-1, P]], channel_multiplier=1).then_inc(s_ident, 1)

            for c in (0, 1, 3):
                n = slice(c * D, (c + 1) * D)
                pool.wait_ge(s_whi, c + 1)
                nc.gpsimd.tensor_tensor(w_lo[:, n], w_raw[:, n], w_hi[:, n].bitcast(fp32), ALU.subtract)\
                  .then_inc(s_wlo, 1)

            def add_bias(t, place, loaded):
                pool.wait_ge(*loaded)
                nc.gpsimd.tensor_tensor(res[:, t, :], x_in[:, place, :], row_buf[:, :], ALU.add).then_inc(s_xb, 1)

            pool.wait_ge(s_bias, 16)
            for t in range(2):
                add_bias(t, t, (s_x_head[t], 16 * G))
            for t in range(2, 4):
                add_bias(t, t, (s_x[1], 16 * G))
            with pool.Fori(0, (NT - 4) // (2 * XS)) as i:
                for e in range(2 * XS):
                    slot = (2 + e // 2) % XS
                    add_bias(2 * XS * i + 4 + e, 2 * slot + e % 2, (s_x[slot], 16 * G * (i + (2 if slot == 1 else 1))))

            nc.gpsimd.memset(col_sum[:, :], 0.0).then_inc(s_cinit, 1)
            nc.gpsimd.memset(same_row[:, :, :], 0.0).then_inc(s_same, 1)
            pool.wait_ge(s_same, 1)
            for c in range(G):
                for q in range(G):
                    part = same_row[:, c, B * c:B * (c + 1)]
                    nc.gpsimd.affine_select(out=part, in_=part, compare_op=ALU.not_equal, fill=1.0, base=-B * q,
                                            pattern=[[-1, B]], channel_multiplier=1).then_inc(s_same, 1)
                    pool.wait_ge(s_same, 2 + G * c + q)

            def add_cols(t, par):
                pool.wait_ge(s_bhi, t + 1)
                nc.gpsimd.tensor_tensor(col_sum[:, :], col_sum[:, :], col_part[:, par, :], ALU.add)\
                  .then_inc(s_csum, 1)
                pool.wait_ge(s_csum, t + 1)

            def copy_x1(t):
                pool.wait_ge(s_x1, t + 1)
                nc.gpsimd.tensor_copy(res[:, t, :], row_buf[:, :]).then_inc(s_res, 1)

            pool.wait_ge(s_cinit, 1)
            add_cols(0, 0)
            add_cols(1, 1)
            with pool.Fori(0, NT // 2 - 1) as i:
                copy_x1(2 * i)
                add_cols(2 * i + 2, 0)
                copy_x1(2 * i + 1)
                add_cols(2 * i + 3, 1)
            copy_x1(NT - 2)
            copy_x1(NT - 1)

        @block.tensor
        def _(pe):
            def product(dst, w, a, first, last):
                nc.tensor.matmul(dst, w[0], a[0], start=first, stop=False)
                nc.tensor.matmul(dst, w[0], a[1], start=False, stop=False)
                return nc.tensor.matmul(dst, w[1], a[0], start=False, stop=last)

            def transpose_h(t, par, reused=True):
                pe.wait_ge(s_h, t + 1)
                if reused:
                    pe.wait_ge(s_hTlo, t - 1)
                for c in range(ND):
                    ins = nc.tensor.transpose(acc[:, HT + par, c * P:(c + 1) * P],
                                              nxt[:, par, c * P:(c + 1) * P], ident[:, :])
                ins.then_inc(s_hT, 1)

            def support(t, par, reused=True, first=False, between=None):
                pe.wait_ge(s_hThi, t + 1)
                pe.wait_ge(s_hTlo, t + 1)
                if reused:
                    pe.wait_ge(s_alo, t - 1)
                for c in range(ND):
                    if between is not None and c == 1:
                        between()
                    k, n = slice(c * P, (c + 1) * P), slice(c * D, (c + 1) * D)
                    if first:
                        pe.wait_ge(s_whi, c + 1)
                        if c == 2:
                            pe.wait_ge(s_wlo2, 1)
                        else:
                            pe.wait_ge(s_wlo, min(c + 1, ND - 1))
                    ins = product(acc[:, par, :], (hT_hi[:, par, k], hT_lo[:, par, k]),
                                  (w_hi[:, n], w_lo[:, n]), c == 0, c == ND - 1)
                ins.then_inc(s_sup, 1)

            def act_tile(k):
                return act_hi[:, k, :], act_lo[:, k, :]

            def aggregate(split, bank, par, fresh=None, release=False, head=None):
                if head is not None:
                    pe.wait_ge(s_hi_head, head[0])
                    pe.wait_ge(s_lo_head, head[1])
                else:
                    pe.wait_ge(s_bhi, split)
                    pe.wait_ge(s_blo, split)
                for k in range(NT):
                    if head is not None and k == HEAD_BLOCKS:
                        pe.wait_ge(s_bhi, split)
                        pe.wait_ge(s_blo, split)
                    if fresh is not None:
                        pe.wait_ge(s_ahi, fresh + k + 1)
                        pe.wait_ge(s_alo, fresh + k + 1)
                    m = slice(k * P, (k + 1) * P)
                    ins = product(acc[:, bank, :], (blk_hi[:, par, m], blk_lo[:, par, m]), act_tile(k),
                                  k == 0, k == NT - 1)
                    if release and k < NT - 1:
                        ins.then_inc(s_used, 1)
                ins.then_inc(s_acc, 1)

            pe.wait_ge(s_ident, 4)
            for _ in range(WARM_UP):
                nc.tensor.matmul(acc[:, SUM, 0:P], ident[:, :], ident[:, :], start=True, stop=True)
            transpose_h(0, 0, False)
            support(0, 0, False, first=True, between=lambda: transpose_h(1, 1, False))
            support(1, 1, False)
            transpose_h(2, 0)
            with pe.Fori(0, NT // 2 - 2) as i:
                transpose_h(2 * i + 3, 1)
                support(2 * i + 2, 0)
                transpose_h(2 * i + 4, 0)
                support(2 * i + 3, 1)
            transpose_h(NT - 1, 1)
            support(NT - 2, 0)
            support(NT - 1, 1)

            pe.wait_ge(s_alo, NT - 1)
            aggregate(1, 0, 0, fresh=0, head=(2, 1))
            aggregate(2, 1, 1, head=(3, 2))

            def layer1(t, par):
                pe.wait_ge(s_x1, t - 1)
                aggregate(t + 1, par, par)

            with pe.Fori(1, NT // 2 - 1) as i:
                layer1(2 * i, 0)
                layer1(2 * i + 1, 1)
            layer1(NT - 2, 0)
            pe.wait_ge(s_same, 1 + G * G)
            pe.wait_ge(s_rsum, NT)
            for c in range(G):
                ins = nc.tensor.matmul(acc[:, SUM, 0:NT], same_row[:, c, :], row_part[:, :, c],
                                       start=c == 0, stop=c == G - 1)
            ins.then_inc(s_rtot, 1)
            pe.wait_ge(s_x1, NT - 2)
            aggregate(NT, 1, 1, release=True)

            def unit_products(half, k, s, bank_free=None, done=None):
                u = NT * half + k
                pe.wait_ge(s_bhi, SPLIT2 + u + 1)
                pe.wait_ge(s_blo, SPLIT2 + u + 1)
                if half == 0:
                    pe.wait_ge(s_ahi, NT + k + 1)
                    pe.wait_ge(s_alo, NT + k + 1)
                for i in range(H):
                    if bank_free is not None:
                        bank_free(i)
                    m = slice(i * P, (i + 1) * P)
                    ins = product(acc[:, (FIRST + i) % 8, :], (unit(blk_hi, s)[:, m], unit(blk_lo, s)[:, m]),
                                  act_tile(k), bank_free is not None, done is not None)
                    if done is not None:
                        ins.then_inc(done, 1)
                if done is None:
                    ins.then_inc(s_unit, 1)

            def free_first(i):
                if (FIRST + i) % 8 == SUM:
                    pe.wait_ge(s_dvar, 1)
                if (FIRST + i) % 8 == 0:
                    pe.wait_ge(s_x1, NT - 1)
                if (FIRST + i) % 8 == 1:
                    pe.wait_ge(s_x1, NT)

            def free_second(i):
                pe.wait_ge(s_z, i + 1)

            for half, bank_free in ((0, free_first), (1, free_second)):
                unit_products(half, 0, 0, bank_free=bank_free)
                with pe.Fori(0, NT // S - 1) as i:
                    for s in range(S):
                        unit_products(half, S * i + s + 1, (s + 1) % S)
                unit_products(half, NT - 3, 1)
                unit_products(half, NT - 2, 2)
                unit_products(half, NT - 1, 3, done=s_acc)

            pe.wait_ge(s_z, H + 1)
            aggregate(SPLIT3 + 1, FIRST, 0, fresh=2 * NT)
            aggregate(SPLIT3 + 2, FIRST + 1, 1)
            with pe.Fori(1, NT // 2) as i:
                pe.wait_ge(s_o, 2 * i - 1)
                aggregate(SPLIT3 + 2 * i + 1, FIRST, 0)
                pe.wait_ge(s_o, 2 * i)
                aggregate(SPLIT3 + 2 * i + 2, FIRST + 1, 1)

        @block.scalar
        def _(act):
            def root(n, c0, c1):
                act.wait_ge(s_var, n + 1)
                nc.scalar.activation(ln_t[:, 1, c0:c1], ln_t[:, 0, c0:c1], ACT.Sqrt).then_inc(s_root, 1)

            def normalize(t, place, n, reused=True):
                par = place % 2
                act.wait_ge(s_norm, n + 1)
                if reused:
                    act.wait_ge(s_hT, t - 1)
                nc.scalar.activation(nxt[:, par, :], x_in[:, place, :], ACT.Relu, scale=rstd[:, par:par + 1],
                                     bias=shift[:, par:par + 1]).then_inc(s_h, 1)

            def split_hT(t, par):
                act.wait_ge(s_hT, t + 1)
                nc.scalar.copy(hT_hi[:, par, :], acc[:, HT + par, :]).then_inc(s_hThi, 1)

            def split_support(t, par):
                act.wait_ge(s_sup, t + 1)
                nc.scalar.copy(act_hi[:, t, :], acc[:, par, :]).then_inc(s_ahi, 1)

            def split_rows(t, par, used=None, blocks=(0, NT), done=None):
                if blocks[1] <= NT // 2:
                    act.wait_ge(s_trn_half, 1)
                else:
                    act.wait_ge(s_trn, t + 1)
                if used is not None:
                    act.wait_ge(s_acc, used)
                    act.wait_ge(s_csum, t - 1)
                for k in range(*blocks):
                    m = slice(k * P, (k + 1) * P)
                    ins = nc.scalar.activation(blk_hi[:, par, m], tr[:, par, m], ACT.Copy,
                                               accum_out=col_part[:, par, k:k + 1])
                ins.then_inc(s_bhi if done is None else done, 1)

            def sum_rows(t, par, loads):
                act.wait_ge(s_nat[par], 16 * G * loads)
                if not isinstance(t, int) or t > 0:
                    act.wait_ge(s_rsum, t)
                for c in range(G):
                    ins = nc.scalar.activation(acc[:, JUNK[c], :], nat[:, par, c * W:(c + 1) * W], ACT.Copy,
                                               accum_out=row_part[:, t, c:c + 1])
                ins.then_inc(s_rsum, 1)

            def normalize1(t):
                act.wait_ge(s_norm, NT // 2 + 1 + t + 1)
                nc.scalar.activation(nxt[:, t, :], row_buf[:, :], ACT.Relu, scale=rstd[:, 0:1],
                                     bias=shift[:, 0:1]).then_inc(s_h1, 1)

            def root1(t):
                root(NT // 2 + 1 + t, 0, 1)

            def split_weight(c):
                act.wait_ge(s_w[min(c, 1)], 16)
                n = slice(c * D, (c + 1) * D)
                nc.scalar.copy(w_hi[:, n], w_raw[:, n]).then_inc(s_whi, 1)

            root(0, 0, 1)
            split_weight(0)
            normalize(0, 0, 0, False)
            root(1, 1, 2)
            split_hT(0, 0)
            split_weight(1)
            split_weight(2)
            normalize(1, 1, 1, False)
            split_weight(3)
            split_hT(1, 1)
            root(2, 0, 2)

            def step(t, e, n=None, roots=True, blocks=None):
                if n is not None:
                    normalize(t + 2, (e + 2) % (2 * XS), n)
                if roots and e % 2:
                    root(n + 1, 0, 2)
                if blocks is not None:
                    split_rows(0, 0, blocks=blocks, done=s_hi_head)
                split_support(t, e % 2)
                if n is not None:
                    split_hT(t + 2, e % 2)

            with act.Fori(0, (NT - 4) // (2 * XS)) as i:
                for e in range(2 * XS):
                    step(2 * XS * i + e, e, XS * i + 1 + e // 2 + 1)
            step(NT - 4, 0, NT // 2, False)
            step(NT - 3, 1, NT // 2, False, (0, HEAD_BLOCKS // 2))
            step(NT - 2, 2, None, False, (HEAD_BLOCKS // 2, HEAD_BLOCKS))
            split_support(NT - 1, 1)
            split_rows(0, 0, blocks=(HEAD_BLOCKS, NT))
            sum_rows(0, 0, 1)

            act.wait_ge(s_sup, NT)
            split_rows(1, 1, blocks=(0, HEAD_BLOCKS), done=s_hi_head)
            split_rows(1, 1, blocks=(HEAD_BLOCKS, NT))
            sum_rows(1, 1, 1)
            split_rows(2, 0, 1)
            root1(0)
            sum_rows(2, 0, 2)
            sum_rows(3, 1, 2)
            normalize1(0)
            with act.Fori(1, NT // 2 - 1) as i:
                split_rows(2 * i + 1, 1, 2 * i)
                root1(2 * i - 1)
                sum_rows(2 * i + 2, 0, i + 2)
                normalize1(2 * i - 1)
                split_rows(2 * i + 2, 0, 2 * i + 1)
                root1(2 * i)
                sum_rows(2 * i + 3, 1, i + 2)
                normalize1(2 * i)
            split_rows(NT - 1, 1, NT - 2)
            root1(NT - 3)
            normalize1(NT - 3)

            def split_unit(u, s, used):
                act.wait_ge(s_sym, u + 1)
                act.wait_ge(*used)
                nc.scalar.copy(unit(blk_hi, s), unit(tr, s)).then_inc(s_bhi, 1)

            def split_g(k, used=None):
                if used is not None:
                    act.wait_ge(s_used, used)
                act.wait_ge(s_h1, k + 1)
                nc.scalar.activation(act_hi[:, k, :], nxt[:, k, :], ACT.Copy, scale=dinv[:, bass.ds(k, 1)])\
                  .then_inc(s_ahi, 1)

            root1(NT - 2)
            act.wait_ge(s_dvar, 1)
            nc.scalar.activation(deg_t[:, 0, :], deg_c[:, :], ACT.Sqrt).then_inc(s_droot, 1)
            split_unit(0, 0, (s_acc, NT - 1))
            normalize1(NT - 2)
            act.wait_ge(s_dinv, 1)
            split_g(0, 1)
            split_unit(1, 1, (s_acc, NT - 1))
            split_g(1, 2)
            root1(NT - 1)
            split_unit(2, 2, (s_acc, NT))
            normalize1(NT - 1)
            split_g(2)
            split_unit(3, 3, (s_acc, NT))
            split_g(3)
            with act.Fori(1, NT // S) as i:
                for s in range(S):
                    split_unit(S * i + s, s, (s_unit, S * i + s - S + 1))
                    split_g(S * i + s)

            def take_z(u, bank):
                act.wait_ge(s_acc, TILE2 + u + 1)
                nc.scalar.activation(nxt[:, u, :], acc[:, bank % 8, :], ACT.Copy,
                                     scale=half_dinv[:, bass.ds(u, 1)]).then_inc(s_z, 1)

            for s in range(S - 1):
                split_unit(NT + s, s, (s_unit, NT - S + s + 1))
            act.wait_ge(s_alo, 2 * NT)
            for t in range(H):
                take_z(t, FIRST + t)
            split_unit(NT + S - 1, S - 1, (s_acc, NT + H))
            with act.Fori(1, NT // S) as i:
                for s in range(S):
                    split_unit(NT + S * i + s, s, (s_unit, NT + S * i + s - S))

            def split_z(k):
                act.wait_ge(s_z, k + 1)
                nc.scalar.copy(act_hi[:, k, :], nxt[:, k, :]).then_inc(s_ahi, 1)

            def split_kept(v, par, loads, used):
                act.wait_ge(s_tr[par], 16 * loads)
                act.wait_ge(*used)
                nc.scalar.copy(blk_hi[:, par, :], tr[:, par, :]).then_inc(s_bhi, 1)

            with act.Fori(0, H) as k:
                act.wait_ge(s_unit, NT + k)
                split_z(k)
            split_kept(0, 0, 1, (s_unit, 2 * NT - 3))
            for k in range(H, NT):
                take_z(k, FIRST + k - H)
                if k < NT - 1:
                    act.wait_ge(s_unit, NT + k)
                split_z(k)
            split_kept(1, 1, 1, (s_acc, TILE3))

            with act.Fori(1, NT // 2) as i:
                split_kept(2 * i, 0, i + 1, (s_acc, TILE3 + 2 * i - 1))
                split_kept(2 * i + 1, 1, i + 1, (s_acc, TILE3 + 2 * i))

        @block.vector
        def _(dve):
            STATS, NORM = 2, 4
            PAIR = 2 * STATS + NORM
            TILE = STATS + NORM
            HEAD = 2 * (STATS + NORM) - PAIR
            BASE1 = HEAD + (NT // 2) * PAIR

            def chained(ins, n):
                ins.then_inc(s_ch, 1)
                dve.wait_ge(s_ch, n)

            def tile_stats(tile, col, n):
                dve.nop(nofuse=True)
                chained(nc.vector.bn_stats(stats[:, col, :], tile), n + 1)
                dve.nop(nofuse=True)
                chained(nc.vector.bn_aggr(mv[:, col, :], stats[:, col, :]), n + 2)

            def variance(c0, c1):
                nc.vector.tensor_scalar(ln_t[:, 0, c0:c1], mv[:, c0:c1, 1], EPS, None, ALU.add)\
                  .then_inc(s_var, 1)

            def inv_root(out_, v, r, a, b, n):
                chained(nc.vector.reciprocal(r, r), n + 1)
                chained(nc.vector.tensor_tensor(a, r, r, ALU.mult), n + 2)
                chained(nc.vector.scalar_tensor_tensor(b, a, -0.5, v, ALU.mult, ALU.mult), n + 3)
                chained(nc.vector.scalar_tensor_tensor(out_, b, 1.5, r, ALU.add, ALU.mult), n + 4)

            def norm(step, c0, c1, n):
                dve.wait_ge(s_root, step + 1)
                c = slice(c0, c1)
                inv_root(rstd[:, c], ln_t[:, 0, c], ln_t[:, 1, c], ln_t[:, 2, c], ln_t[:, 3, c], n)
                nc.vector.scalar_tensor_tensor(shift[:, c], mv[:, c, 0], -1.0, rstd[:, c],
                                               ALU.mult, ALU.mult).then_inc(s_norm, 1)

            def split_hT(t, par):
                dve.wait_ge(s_hThi, t + 1)
                nc.vector.tensor_tensor(hT_lo[:, par, :], acc[:, HT + par, :], hT_hi[:, par, :].bitcast(fp32),
                                        ALU.subtract).then_inc(s_hTlo, 1)

            def split_support(t, par):
                dve.wait_ge(s_ahi, t + 1)
                nc.vector.tensor_tensor(act_lo[:, t, :], acc[:, par, :], act_hi[:, t, :].bitcast(fp32),
                                        ALU.subtract).then_inc(s_alo, 1)

            def transpose_rows(t, par, j, blocks=(0, NT)):
                dve.wait_ge(s_nat[par], 16 * G * (j + 1))
                if not isinstance(t, int) or t > 1:
                    dve.wait_ge(s_keep[par], 16 * j)
                    dve.wait_ge(s_blo, t - 1)
                b0, b1 = blocks
                ins = nc.vector.transpose(
                    tr[:, par, b0 * P:b1 * P].rearrange("p (k c b) -> p c k b", c=G, b=B),
                    nat[:, par, :].rearrange("p (c k a) -> p c k a", c=G, a=B)[:, :, b0:b1, :])
                ins.then_inc(s_trn if b1 == NT else s_trn_half, 1)

            def split_block(n, hi, lo, raw):
                dve.wait_ge(s_bhi, n + 1)
                nc.vector.tensor_tensor(lo, raw, hi.bitcast(fp32), ALU.subtract).then_inc(s_blo, 1)

            def split_tile(n, par):
                split_block(n, blk_hi[:, par, :], blk_lo[:, par, :], tr[:, par, :])

            def split_head(t, parts):
                m = slice(0, HEAD_BLOCKS * P)
                dve.wait_ge(s_hi_head, parts)
                nc.vector.tensor_tensor(blk_lo[:, t, m], tr[:, t, m], blk_hi[:, t, m].bitcast(fp32), ALU.subtract)\
                  .then_inc(s_lo_head, 1)

            def split_rest(t):
                m = slice(HEAD_BLOCKS * P, N)
                split_block(t, blk_hi[:, t, m], blk_lo[:, t, m], tr[:, t, m])

            def take_x1(t, par, n):
                dve.wait_ge(s_acc, t + 1)
                if not isinstance(t, int) or t > 0:
                    dve.wait_ge(s_h1, t)
                    dve.wait_ge(s_res, t)
                nc.vector.tensor_tensor(row_buf[:, :], acc[:, par, :], res[:, t, :], ALU.add).then_inc(s_x1, 1)
                dve.wait_ge(s_x1, t + 1)
                tile_stats(row_buf[:, :], 0, n)
                variance(0, 1)

            def norm1(t, n):
                norm(NT // 2 + 1 + t, 0, 1, n)

            for t in range(2):
                dve.wait_ge(s_x_head[t], 16 * G)
                tile_stats(x_in[:, t, :], t, (STATS + NORM) * t)
                variance(t, t + 1)
                norm(t, t, t + 1, (STATS + NORM) * t + STATS)
            split_hT(0, 0)
            dve.wait_ge(s_whi, 3)
            n = slice(2 * D, 3 * D)
            nc.vector.tensor_tensor(w_lo[:, n], w_raw[:, n], w_hi[:, n].bitcast(fp32), ALU.subtract)\
              .then_inc(s_wlo2, 1)
            dve.wait_ge(s_x[1], 16 * G)
            dve.wait_ge(s_h, 2)
            tile_stats(x_in[:, 2, :], 0, HEAD + PAIR)
            split_hT(1, 1)
            tile_stats(x_in[:, 3, :], 1, HEAD + PAIR + STATS)
            variance(0, 2)
            norm(2, 0, 2, HEAD + PAIR + 2 * STATS)

            with dve.Fori(0, (NT - 4) // (2 * XS)) as i:
                for e in range(2 * XS):
                    t, j = 2 * XS * i + e, XS * i + 2 + e // 2
                    slot = (2 + e // 2) % XS
                    n = HEAD + PAIR * j
                    if e % 2 == 0:
                        dve.wait_ge(s_x[slot], 16 * G * (i + (2 if slot == 1 else 1)))
                    tile_stats(x_in[:, 2 * slot + e % 2, :], e % 2, n + STATS * (e % 2))
                    if e % 2:
                        variance(0, 2)
                    if e % 2:
                        norm(j + 1, 0, 2, n + 2 * STATS)
                    split_support(t, e % 2)
                    split_hT(t + 2, e % 2)
            transpose_rows(0, 0, 0, (0, NT // 2))
            split_support(NT - 4, 0)
            split_hT(NT - 2, 0)
            transpose_rows(0, 0, 0, (NT // 2, NT))
            split_support(NT - 3, 1)
            split_hT(NT - 1, 1)
            split_head(0, 2)
            split_support(NT - 2, 0)
            split_support(NT - 1, 1)
            split_rest(0)
            transpose_rows(1, 1, 0)

            dve.wait_ge(s_xb, NT)
            split_head(1, 3)
            split_rest(1)
            transpose_rows(2, 0, 1)

            def layer1(t, par, j, n):
                take_x1(t - 1, 1 - par, n)
                transpose_rows(t + 2, par, j + 1)
                split_tile(t + 1, 1 - par)
                norm1(t - 1, n + STATS)

            take_x1(0, 0, BASE1)
            split_tile(2, 0)
            norm1(0, BASE1 + STATS)
            transpose_rows(3, 1, 1)
            with dve.Fori(1, NT // 2 - 1) as i:
                layer1(2 * i, 0, i, BASE1 + TILE * (2 * i - 1))
                layer1(2 * i + 1, 1, i, BASE1 + TILE * (2 * i))
            n = BASE1 + TILE * (NT - 3)
            take_x1(NT - 3, 1, n)
            split_tile(NT - 1, 1)
            norm1(NT - 3, n + STATS)

            def symmetric(half, s, loads, diag=None):
                dve.wait_ge(s_natu[s], 16 * G * loads)
                dve.wait_ge(s_tru[s], 16 * loads)
                blocks = unit(tr, s).rearrange("p (t q b) -> p t q b", q=G, b=B)
                ins = nc.vector.tensor_tensor(blocks, blocks,
                                              unit(nat, s).rearrange("p (q t b) -> p t q b", q=G, b=B), ALU.add)
                if diag is None:
                    ins.then_inc(s_sym, 1)
                else:
                    ins.then_inc(s_sadd, 1)
                    dve.wait_ge(s_sadd, diag + 1 + H * half)
                    own = unit(tr, s)[:, bass.ds(P * diag, P)]
                    nc.vector.tensor_tensor(own, own, ident2[:, :], ALU.add).then_inc(s_sym, 1)

            def split_unit(u, s):
                split_block(SPLIT2 + u, unit(blk_hi, s), unit(blk_lo, s), unit(tr, s))

            def split_g(k):
                dve.wait_ge(s_ahi, NT + k + 1)
                nc.vector.scalar_tensor_tensor(act_lo[:, k, :], nxt[:, k, :], dinv[:, bass.ds(k, 1)],
                                               act_hi[:, k, :].bitcast(fp32), ALU.mult, ALU.subtract)\
                  .then_inc(s_alo, 1)

            n = BASE1 + TILE * (NT - 2)
            take_x1(NT - 2, 0, n)
            dve.wait_ge(s_csum, NT)
            dve.wait_ge(s_rtot, 1)
            chained(nc.vector.tensor_tensor(deg[:, :], acc[:, SUM, 0:NT], col_sum[:, :], ALU.add), n + STATS + 1)
            chained(nc.vector.tensor_scalar(deg[:, :], deg[:, :], 0.5, 1.0, ALU.mult, ALU.add), n + STATS + 2)
            chained(nc.vector.tensor_scalar(deg_pos[:, :], deg[:, :], 0.0, None, ALU.is_gt), n + STATS + 3)
            nc.vector.tensor_scalar(deg_c[:, :], deg[:, :], 2.0 ** -100, None, ALU.max).then_inc(s_dvar, 1)
            n += STATS + 3
            symmetric(0, 0, 1, 0)
            dve.wait_ge(s_droot, 1)
            inv_root(deg_t[:, 1, :], deg_c[:, :], deg_t[:, 0, :], deg_t[:, 2, :], deg_t[:, 3, :], n)
            chained(nc.vector.tensor_tensor(dinv[:, :], deg_t[:, 1, :], deg_pos[:, :], ALU.mult), n + 5)
            nc.vector.tensor_scalar(half_dinv[:, :], dinv[:, :], 0.5, None, ALU.mult).then_inc(s_dinv, 1)
            norm1(NT - 2, n + 5)
            n += 5 + NORM
            symmetric(0, 1, 1, 1)
            split_unit(0, 0)
            split_g(0)
            split_unit(1, 1)
            split_g(1)
            symmetric(0, 2, 1, 2)
            take_x1(NT - 1, 1, n)
            symmetric(0, 3, 1, 3)
            norm1(NT - 1, n + STATS)
            split_unit(2, 2)
            split_g(2)
            split_unit(3, 3)
            split_g(3)

            def units(half, j, diag):
                u, loads = NT * half + S * j, NT // S * half + j + 1
                own = [S * j + s - (H if half else 0) if diag else None for s in range(S)]
                symmetric(half, 0, loads, own[0])
                for s in range(S):
                    if s < S - 1:
                        symmetric(half, s + 1, loads, own[s + 1])
                    split_unit(u + s, s)
                    if half == 0:
                        split_g(S * j + s)

            units(0, 1, True)
            with dve.Fori(H // S, NT // S) as i:
                units(0, i, False)
            with dve.Fori(0, H // S) as i:
                units(1, i, False)
            with dve.Fori(H // S, NT // S) as i:
                units(1, i, True)

            def split_z(k):
                dve.wait_ge(s_ahi, 2 * NT + k + 1)
                nc.vector.tensor_tensor(act_lo[:, k, :], nxt[:, k, :], act_hi[:, k, :].bitcast(fp32),
                                        ALU.subtract).then_inc(s_alo, 1)

            with dve.Fori(0, H) as k:
                split_z(k)
            split_tile(SPLIT3, 0)
            with dve.Fori(H, NT) as k:
                split_z(k)
            split_tile(SPLIT3 + 1, 1)

            def take_out(v, bank):
                dve.wait_ge(s_acc, TILE3 + v + 1)
                nc.vector.tensor_tensor(res[:, v, :], acc[:, bank, :], res[:, v, :], ALU.add).then_inc(s_o, 1)

            dve.wait_ge(s_res, NT)
            with dve.Fori(1, NT // 2) as i:
                take_out(2 * i - 2, FIRST)
                split_tile(SPLIT3 + 2 * i, 0)
                take_out(2 * i - 1, FIRST + 1)
                split_tile(SPLIT3 + 2 * i + 1, 1)
            take_out(NT - 2, FIRST)
            take_out(NT - 1, FIRST + 1)


_INS = ['x', 'adj', 'L0_gnn_weight', 'L0_gnn_bias']


def kernel(**inputs):
    import numpy as _np
    import concourse.bacc as _bacc
    from concourse import mybir as _mybir
    from concourse.bass_utils import run_bass_kernel_spmd as _run

    nc = _bacc.Bacc("TRN2", target_bir_lowering=False, num_devices=1)
    arrays, args = {}, []
    for name in _INS:
        a = _np.ascontiguousarray(inputs[name])
        arrays[f"in_{name}_dram"] = a
        args.append(nc.dram_tensor(f"in_{name}_dram", a.shape, _mybir.dt.from_np(a.dtype), kind="ExternalInput").ap())
    shape = inputs['x'].shape
    rows = inputs['adj'].shape[0]
    kept = nc.dram_tensor("adj_t_blocks", (rows // 128, 128, rows), _mybir.dt.float32, kind="Internal").ap()
    result = nc.dram_tensor("out_dram", shape, _mybir.dt.float32, kind="ExternalOutput").ap()
    two_layer_graph_conv(nc, *args, kept, result)
    r = _run(nc, [arrays], core_ids=[0])
    return r.results[0]["out_dram"]
```
